# Optimizing a Trainium2 kernel written in Bass

```python
import numpy as np
import jax
import jax.numpy as jnp

def _softmax(x, axis=-1):
    return jax.nn.softmax(x, axis=axis)

def _gelu(x):
    return jax.nn.gelu(x, approximate=True)

def _silu(x):
    return jax.nn.silu(x)

def _sigmoid(x):
    return jax.nn.sigmoid(x)

def _layernorm(x, axis=-1, eps=1e-05):
    m = jnp.mean(x, axis=axis, keepdims=True)
    v = jnp.var(x, axis=axis, keepdims=True)
    return (x - m) / jnp.sqrt(v + eps)

def _scatter_add(tgt, idx, src, axis=0):
    return tgt.at[idx].add(src)

def _segment_sum(src, seg, n):
    return jax.ops.segment_sum(src, seg, n)
kernel_name = 'mk_cond_seq_d2_seqx_r8_a44a9b'

def setup_inputs(seed: int=0):
    np.random.seed(seed)
    _w = jnp.asarray

    def _rec_inputs():
        import jax
        import jax.numpy as jnp
        _rk = jax.random.key(seed)
        x = 7.22e-05 + 1 * jax.random.normal(jax.random.fold_in(_rk, 1), (16, 128, 128), jnp.float32)
        _lenS = 128 - jax.random.randint(jax.random.fold_in(_rk, 7), (16,), 0, max(1, 128 // 4) + 1, jnp.int32)
        _lenS2 = 128 - jax.random.randint(jax.random.fold_in(_rk, 8), (16,), 0, max(1, 128 // 4) + 1, jnp.int32)
        cond_1024 = 0.0061147 + 1.02565 * jax.random.normal(jax.random.fold_in(_rk, 11), (16, 128), jnp.float32)
        _validS = jnp.arange(128)[None, :] < _lenS[:, None]
        _validS2 = jnp.arange(128)[None, :] < _lenS2[:, None]
        _causal = jnp.tril(jnp.ones((128, 128), dtype=bool))
        mask_BxS_bk1 = jnp.broadcast_to(_validS[:, :], (16, 128))
        return (x, cond_1024, mask_BxS_bk1)
    x, cond_1024, mask_BxS_bk1 = _rec_inputs()

    def _L0_cond_setup():
        import jax, jax.numpy as jnp
        import numpy as np
        DIM = 128
        MLP_RATIO = 4
        EPS = 1e-06

        def rmsnorm(x, w):
            return x * jax.lax.rsqrt(jnp.mean(x * x, axis=-1, keepdims=True) + EPS) * w

        def film(x, cond, w, b):
            ss = cond @ w + b
            scale, shift = jnp.split(ss, 2, axis=-1)
            return x * (1.0 + scale[:, None, :]) + shift[:, None, :]
        key = jax.random.key(seed)
        ks = jax.random.split(key, 16)
        B, N, D = (4, 256, DIM)
        H = D * MLP_RATIO
        s = lambda fan_in: 1.0 / np.sqrt(fan_in)
        return {'x': jax.random.normal(ks[0], (B, N, D), jnp.float32), 'cond': jax.random.normal(ks[1], (B, D), jnp.float32), 'norm1_w': jnp.ones((D,), jnp.float32), 'film1_w': jax.random.normal(ks[2], (D, 2 * D), jnp.float32) * s(D), 'film1_b': jnp.zeros((2 * D,), jnp.float32), 'q_w': jax.random.normal(ks[3], (D, D), jnp.float32) * s(D), 'q_b': jnp.zeros((D,), jnp.float32), 'k_w': jax.random.normal(ks[4], (D, D), jnp.float32) * s(D), 'k_b': jnp.zeros((D,), jnp.float32), 'v_w': jax.random.normal(ks[5], (D, D), jnp.float32) * s(D), 'v_b': jnp.zeros((D,), jnp.float32), 'proj_w': jax.random.normal(ks[6], (D, D), jnp.float32) * s(D), 'proj_b': jnp.zeros((D,), jnp.float32), 'norm2_w': jnp.ones((D,), jnp.float32), 'film2_w': jax.random.normal(ks[7], (D, 2 * D), jnp.float32) * s(D), 'film2_b': jnp.zeros((2 * D,), jnp.float32), 'mlp_w1': jax.random.normal(ks[8], (D, H), jnp.float32) * s(D), 'mlp_b1': jnp.zeros((H,), jnp.float32), 'mlp_w2': jax.random.normal(ks[9], (H, D), jnp.float32) * s(H), 'mlp_b2': jnp.zeros((D,), jnp.float32)}
    _L0_cond_all = _L0_cond_setup()
    _L0_cond_in = {k: v for k, v in _L0_cond_all.items() if k in ('norm1_w', 'film1_w', 'film1_b', 'q_w', 'q_b', 'k_w', 'k_b', 'v_w', 'v_b', 'proj_w', 'proj_b', 'norm2_w', 'film2_w', 'film2_b', 'mlp_w1', 'mlp_b1', 'mlp_w2', 'mlp_b2')}
    del _L0_cond_all

    def _L1_cond_setup():
        import jax, jax.numpy as jnp
        import numpy as np
        B, N, C = (8, 128, 128)
        H = 16
        HD = C // H
        MLP = 4 * C
        EPS = 1e-06

        def _layernorm(x):
            mu = jnp.mean(x, axis=-1, keepdims=True)
            var = jnp.mean((x - mu) ** 2, axis=-1, keepdims=True)
            return (x - mu) * jax.lax.rsqrt(var + EPS)

        def _modulate(x, shift, scale):
            return x * (1.0 + scale[:, None, :]) + shift[:, None, :]

        def _attention(x, padding_mask, qkv_w, qkv_b, proj_w, proj_b):
            b, n, cdim = x.shape
            qkv = x @ qkv_w.T + qkv_b
            qkv = qkv.reshape(b, n, 3, H, HD).transpose(2, 0, 3, 1, 4)
            q, k, v = (qkv[0], qkv[1], qkv[2])
            scale = HD ** (-0.5)
            attn = jnp.einsum('bhnd,bhmd->bhnm', q, k) * scale
            mask = padding_mask[:, None, :] & padding_mask[:, :, None]
            attn = jnp.where(mask[:, None, :, :], attn, -1000000000.0)
            attn = jax.nn.softmax(attn, axis=-1)
            out = jnp.einsum('bhnm,bhmd->bhnd', attn, v)
            out = out.transpose(0, 2, 1, 3).reshape(b, n, cdim)
            return out @ proj_w.T + proj_b
        key = jax.random.key(seed)
        ks = jax.random.split(key, 12)
        x = jax.random.normal(ks[0], (B, N, C), dtype=jnp.float32)
        c = jax.random.normal(ks[1], (B, C), dtype=jnp.float32)
        lengths = jax.random.randint(ks[2], (B,), N // 2, N + 1)
        padding_mask = jnp.arange(N)[None, :] < lengths[:, None]
        s = 0.02
        qkv_w = jax.random.normal(ks[3], (3 * C, C), dtype=jnp.float32) * s
        qkv_b = jnp.zeros((3 * C,), dtype=jnp.float32)
        proj_w = jax.random.normal(ks[4], (C, C), dtype=jnp.float32) * s
        proj_b = jnp.zeros((C,), dtype=jnp.float32)
        fc1_w = jax.random.normal(ks[5], (MLP, C), dtype=jnp.float32) * s
        fc1_b = jnp.zeros((MLP,), dtype=jnp.float32)
        fc2_w = jax.random.normal(ks[6], (C, MLP), dtype=jnp.float32) * s
        fc2_b = jnp.zeros((C,), dtype=jnp.float32)
        ada_w = jax.random.normal(ks[7], (6 * C, C), dtype=jnp.float32) * s
        ada_b = jnp.zeros((6 * C,), dtype=jnp.float32)
        return {'x': x, 'c': c, 'padding_mask': padding_mask, 'qkv_w': qkv_w, 'qkv_b': qkv_b, 'proj_w': proj_w, 'proj_b': proj_b, 'fc1_w': fc1_w, 'fc1_b': fc1_b, 'fc2_w': fc2_w, 'fc2_b': fc2_b, 'ada_w': ada_w, 'ada_b': ada_b}
    _L1_cond_all = _L1_cond_setup()
    _L1_cond_in = {k: v for k, v in _L1_cond_all.items() if k in ('qkv_w', 'qkv_b', 'proj_w', 'proj_b', 'fc1_w', 'fc1_b', 'fc2_w', 'fc2_b', 'ada_w', 'ada_b')}
    del _L1_cond_all
    return {'x': x, 'cond_1024': cond_1024, 'mask_BxS_bk1': mask_BxS_bk1, 'L0_cond_norm1_w': _L0_cond_in['norm1_w'], 'L0_cond_film1_w': _L0_cond_in['film1_w'], 'L0_cond_film1_b': _L0_cond_in['film1_b'], 'L0_cond_q_w': _L0_cond_in['q_w'], 'L0_cond_q_b': _L0_cond_in['q_b'], 'L0_cond_k_w': _L0_cond_in['k_w'], 'L0_cond_k_b': _L0_cond_in['k_b'], 'L0_cond_v_w': _L0_cond_in['v_w'], 'L0_cond_v_b': _L0_cond_in['v_b'], 'L0_cond_proj_w': _L0_cond_in['proj_w'], 'L0_cond_proj_b': _L0_cond_in['proj_b'], 'L0_cond_norm2_w': _L0_cond_in['norm2_w'], 'L0_cond_film2_w': _L0_cond_in['film2_w'], 'L0_cond_film2_b': _L0_cond_in['film2_b'], 'L0_cond_mlp_w1': _L0_cond_in['mlp_w1'], 'L0_cond_mlp_b1': _L0_cond_in['mlp_b1'], 'L0_cond_mlp_w2': _L0_cond_in['mlp_w2'], 'L0_cond_mlp_b2': _L0_cond_in['mlp_b2'], 'L1_cond_qkv_w': _L1_cond_in['qkv_w'], 'L1_cond_qkv_b': _L1_cond_in['qkv_b'], 'L1_cond_proj_w': _L1_cond_in['proj_w'], 'L1_cond_proj_b': _L1_cond_in['proj_b'], 'L1_cond_fc1_w': _L1_cond_in['fc1_w'], 'L1_cond_fc1_b': _L1_cond_in['fc1_b'], 'L1_cond_fc2_w': _L1_cond_in['fc2_w'], 'L1_cond_fc2_b': _L1_cond_in['fc2_b'], 'L1_cond_ada_w': _L1_cond_in['ada_w'], 'L1_cond_ada_b': _L1_cond_in['ada_b']}

def reference(x, cond_1024, mask_BxS_bk1, L0_cond_norm1_w, L0_cond_film1_w, L0_cond_film1_b, L0_cond_q_w, L0_cond_q_b, L0_cond_k_w, L0_cond_k_b, L0_cond_v_w, L0_cond_v_b, L0_cond_proj_w, L0_cond_proj_b, L0_cond_norm2_w, L0_cond_film2_w, L0_cond_film2_b, L0_cond_mlp_w1, L0_cond_mlp_b1, L0_cond_mlp_w2, L0_cond_mlp_b2, L1_cond_qkv_w, L1_cond_qkv_b, L1_cond_proj_w, L1_cond_proj_b, L1_cond_fc1_w, L1_cond_fc1_b, L1_cond_fc2_w, L1_cond_fc2_b, L1_cond_ada_w, L1_cond_ada_b):
    import jax
    import jax.numpy as jnp

    def _L0_cond_ref(x, cond, norm1_w, film1_w, film1_b, q_w, q_b, k_w, k_b, v_w, v_b, proj_w, proj_b, norm2_w, film2_w, film2_b, mlp_w1, mlp_b1, mlp_w2, mlp_b2):
        import jax, jax.numpy as jnp
        import numpy as np
        DIM = 128
        MLP_RATIO = 4
        EPS = 1e-06

        def rmsnorm(x, w):
            return x * jax.lax.rsqrt(jnp.mean(x * x, axis=-1, keepdims=True) + EPS) * w

        def film(x, cond, w, b):
            ss = cond @ w + b
            scale, shift = jnp.split(ss, 2, axis=-1)
            return x * (1.0 + scale[:, None, :]) + shift[:, None, :]
        B, N, D = x.shape
        x_in = x
        h = film(rmsnorm(x, norm1_w), cond, film1_w, film1_b)
        Q = h @ q_w + q_b
        K = h @ k_w + k_b
        V = h @ v_w + v_b
        scores = jnp.einsum('bnd,bmd->bnm', Q, K) * D ** (-0.5)
        attn = jax.nn.softmax(scores, axis=-1)
        out = jnp.einsum('bnm,bmd->bnd', attn, V)
        x = x_in + (out @ proj_w + proj_b)
        x_in = x
        h = film(rmsnorm(x, norm2_w), cond, film2_w, film2_b)
        h = jax.nn.gelu(h @ mlp_w1 + mlp_b1, approximate=False) @ mlp_w2 + mlp_b2
        return x_in + h

    def _L1_cond_ref(x, c, padding_mask, qkv_w, qkv_b, proj_w, proj_b, fc1_w, fc1_b, fc2_w, fc2_b, ada_w, ada_b):
        import jax, jax.numpy as jnp
        import numpy as np
        B, N, C = (8, 128, 128)
        H = 16
        HD = C // H
        MLP = 4 * C
        EPS = 1e-06

        def _layernorm(x):
            mu = jnp.mean(x, axis=-1, keepdims=True)
            var = jnp.mean((x - mu) ** 2, axis=-1, keepdims=True)
            return (x - mu) * jax.lax.rsqrt(var + EPS)

        def _modulate(x, shift, scale):
            return x * (1.0 + scale[:, None, :]) + shift[:, None, :]

        def _attention(x, padding_mask, qkv_w, qkv_b, proj_w, proj_b):
            b, n, cdim = x.shape
            qkv = x @ qkv_w.T + qkv_b
            qkv = qkv.reshape(b, n, 3, H, HD).transpose(2, 0, 3, 1, 4)
            q, k, v = (qkv[0], qkv[1], qkv[2])
            scale = HD ** (-0.5)
            attn = jnp.einsum('bhnd,bhmd->bhnm', q, k) * scale
            mask = padding_mask[:, None, :] & padding_mask[:, :, None]
            attn = jnp.where(mask[:, None, :, :], attn, -1000000000.0)
            attn = jax.nn.softmax(attn, axis=-1)
            out = jnp.einsum('bhnm,bhmd->bhnd', attn, v)
            out = out.transpose(0, 2, 1, 3).reshape(b, n, cdim)
            return out @ proj_w.T + proj_b
        mod = jax.nn.silu(c) @ ada_w.T + ada_b
        shift_msa, scale_msa, gate_msa, shift_mlp, scale_mlp, gate_mlp = jnp.split(mod, 6, axis=1)
        h = _modulate(_layernorm(x), shift_msa, scale_msa)
        x = x + gate_msa[:, None, :] * _attention(h, padding_mask, qkv_w, qkv_b, proj_w, proj_b)
        h = _modulate(_layernorm(x), shift_mlp, scale_mlp)
        h = jax.nn.gelu(h @ fc1_w.T + fc1_b, approximate=True) @ fc2_w.T + fc2_b
        x = x + gate_mlp[:, None, :] * h
        return x
    x = _L0_cond_ref(x, cond_1024, L0_cond_norm1_w, L0_cond_film1_w, L0_cond_film1_b, L0_cond_q_w, L0_cond_q_b, L0_cond_k_w, L0_cond_k_b, L0_cond_v_w, L0_cond_v_b, L0_cond_proj_w, L0_cond_proj_b, L0_cond_norm2_w, L0_cond_film2_w, L0_cond_film2_b, L0_cond_mlp_w1, L0_cond_mlp_b1, L0_cond_mlp_w2, L0_cond_mlp_b2)
    x = _L1_cond_ref(x, cond_1024, mask_BxS_bk1, L1_cond_qkv_w, L1_cond_qkv_b, L1_cond_proj_w, L1_cond_proj_b, L1_cond_fc1_w, L1_cond_fc1_b, L1_cond_fc2_w, L1_cond_fc2_b, L1_cond_ada_w, L1_cond_ada_b)
    return x

_drawn_inputs = setup_inputs


def setup_inputs(seed=0):
    import zlib

    import numpy as np

    out = dict(_drawn_inputs(seed))
    spreads = {'L0_cond_norm1_w': (1.0, 0.2),
     'L0_cond_film1_b': (0.0, 0.1),
     'L0_cond_q_b': (0.0, 0.1),
     'L0_cond_k_b': (0.0, 0.8),
     'L0_cond_v_b': (0.0, 0.1),
     'L0_cond_proj_b': (0.0, 0.1),
     'L0_cond_norm2_w': (1.0, 0.2),
     'L0_cond_film2_b': (0.0, 0.1),
     'L0_cond_mlp_b1': (0.0, 0.1),
     'L0_cond_mlp_b2': (0.0, 0.1),
     'L1_cond_qkv_b': (0.0, 0.8),
     'L1_cond_proj_b': (0.0, 0.8),
     'L1_cond_fc1_b': (0.0, 0.8),
     'L1_cond_fc2_b': (0.0, 0.8),
     'L1_cond_ada_b': (0.0, 0.8)}
    factors = {'L1_cond_qkv_w': 8.0,
     'L1_cond_proj_w': 8.0,
     'L1_cond_fc1_w': 8.0,
     'L1_cond_fc2_w': 8.0,
     'L1_cond_ada_w': 5.363}
    for name, (base, spread) in spreads.items():
        noise = np.random.default_rng([zlib.crc32(name.encode()), seed]).standard_normal(out[name].shape)
        drawn = base * np.exp(spread * noise) if base else spread * noise
        out[name] = jnp.asarray(drawn.astype(out[name].dtype))
    for name, factor in factors.items():
        out[name] = (out[name] * factor).astype(out[name].dtype)
    return out
```

```python
from contextlib import ExitStack

import concourse.bass as bass
from concourse import mybir

F32 = mybir.dt.float32
F32R = mybir.dt.float32r
BF16 = mybir.dt.bfloat16
I32 = mybir.dt.int32
ALU = mybir.AluOpType
ACT = mybir.ActivationFunctionType
AX = mybir.AxisListType

B, N, C = 16, 128, 128
H, HD = 16, 8
F = 4 * C
FC = F // C
G = 4
EPS = 1e-6
MASKED = -1e9
ROWS = 32
MROW = 12

_W = [("cond", B), ("film1", 2 * C), ("film2", 2 * C), ("cols0", 16), ("q", C), ("k", C), ("vt", C),
      ("proj", C), ("x_end", 0), ("mlp1", F), ("mlp2", F), ("m_end", 0), ("ada", 6 * C),
      ("cols1", 16), ("qkv", 3 * C), ("proj1", C), ("fc1", F), ("fc2", F)]
W_AT, _n = {}, 0
for _name, _size in _W:
    W_AT[_name] = _n
    _n += _size
W_ALL = _n
_R = [("proj_b", C), ("mlp_b2", C), ("qk_b", 2 * C), ("proj1_b", C), ("fc2_b", C), ("gate_b", 2 * C)]
R_AT, _n = {}, 0
for _name, _size in _R:
    R_AT[_name] = _n
    _n += _size
R_ALL = _n


def build(nc, x, weights, rows, mask, mask_t, gates, out):
    with ExitStack() as ctx:
        def sb(name, shape, dt=F32):
            return ctx.enter_context(nc.sbuf_tensor(name, shape, dt))

        def sem(name):
            return ctx.enter_context(nc.semaphore(name))

        W = sb("W", [128, W_ALL])
        R = sb("R", [128, R_ALL])
        xs = sb("xs", [N, B, C])
        xb = sb("xb", [N, B, C])
        agg = sb("agg", [N, G, 2])
        mean = sb("mean", [N, 2, B])
        rstd = sb("rstd", [N, 4, B])
        var_eps = sb("var_eps", [N, 4, B])
        mean_sq = sb("mean_sq", [N, G])
        bn = sb("bn", [N, G, 6])
        half = sb("half", [N, B])
        ident = sb("ident", [128, 128])
        identb = sb("identb", [128, 128], BF16)
        xn = [sb(f"xn{u}", [N, G, C]) for u in range(2)]
        hT = [sb(f"hT{u}", [C, G, N]) for u in range(2)]
        scale = sb("scale", [C, 4, B])
        shift = sb("shift", [C, 4, B])
        qT = [sb(f"qT{u}", [C, G, N]) for u in range(2)]
        kT = [sb(f"kT{u}", [C, G, N]) for u in range(2)]
        v0 = [sb(f"av{u}", [N, G, C]) for u in range(2)]
        p0 = [sb(f"ap{u}", [N, G, N]) for u in range(2)]
        pT0 = [sb(f"apT{u}", [N, G, N]) for u in range(2)]
        amax = sb("amax", [N, 2, G])
        aden = sb("aden", [N, 2, G])
        arden = sb("arden", [N, 2, G])
        wvp = sb("wvp", [C, C])
        bias_a = sb("bias_a", [N, C])
        bcol = sb("bcol", [C, N])
        hid = [sb(f"hid{u}", [128, FC, G, N]) for u in range(2)]
        gmul = [sb(f"gmul{u}", [N, G, C]) for u in range(2)]
        cond_e = sb("cond_e", [C, B])
        cond_s = sb("cond_s", [C, B])
        cond_r = sb("cond_r", [C, B])
        silu = sb("silu", [C, B])
        gate_rows = sb("gate_rows", [B, 2, C])
        gate = sb("gate", [N, B, 2, C])
        pbias1 = sb("pbias1", [N, C])
        bcol1 = sb("bcol1", [C, N])
        gtmp = sb("gtmp", [N, G, C])
        mask_i = sb("mask_i", [128, B, N], I32)
        maskt_i = sb("maskt_i", [N, B], I32)
        valid = sb("valid", [N, B])
        mod32 = sb("mod32", [128, 32])
        sel_f = sb("sel_f", [128, 4])
        row_amp = sb("row_amp", [128, 1])
        row_neg = sb("row_neg", [128, 1])
        mask_term = sb("mask_term", [128, B, N], BF16)
        sel_base = sb("sel_base", [128, 4, N], BF16)
        pick_mask = sb("pick_mask", [128, N], BF16)
        sel = [sb(f"sel{u}", [128, 4, N], BF16) for u in range(2)]
        xc = [sb(f"xc{u}", [N, C]) for u in range(2)]
        hc = [sb(f"hc{u}", [C, N]) for u in range(2)]
        qbv = [sb(f"qbv{u}", [N, C]) for u in range(2)]
        qk = [sb(f"qk{u}", [N, 2, H, HD]) for u in range(2)]
        qkx = [sb(f"qkx{u}", [N, 2, H, 4, HD]) for u in range(2)]
        qxT = [sb(f"qxT{u}", [128, 4, N], F32R) for u in range(2)]
        kxT = [sb(f"kxT{u}", [128, 4, N], F32R) for u in range(2)]
        vx = [sb(f"vx{u}", [N, 8 * 64]) for u in range(2)]
        nmax = [sb(f"nmax{u}", [N, 16]) for u in range(2)]
        mrest = [sb(f"mrest{u}", [N, 16]) for u in range(2)]
        nm = [sb(f"nm{u}", [N, 4, 32], BF16) for u in range(2)]
        nmT = [sb(f"nmT{u}", [128, N], BF16) for u in range(2)]
        pT = [sb(f"pT{u}", [N, 4, 4, N]) for u in range(2)]
        oT = [sb(f"oT{u}", [128, 2, N]) for u in range(2)]
        rden = [sb(f"rden{u}", [N, 16]) for u in range(2)]
        on = [sb(f"on{u}", [N, 16, HD]) for u in range(2)]
        onT = [sb(f"onT{u}", [C, N]) for u in range(2)]
        attn = [sb(f"attn{u}", [N, C]) for u in range(2)]

        ps = ctx.enter_context(nc.psum_tensor("ps", [128, 8, 512], F32))

        def bank(i):
            return ps[:, i, :].rearrange("p (g n) -> p g n", g=G)

        def w(name, size=C, at=0):
            a = W_AT[name] + at
            return W[:, a:a + size]

        def row(name, size=C, at=0):
            a = R_AT[name] + at
            return R[:, a:a + size]

        def col(name, j):
            return w(name, 1, j)

        COL = {"q_b": 0, "k_b": 1, "v_b": 2, "n1": 3, "n2": 4, "film1": 5, "film2": 7, "mlp_b1": 9}
        COL1 = {"ada": 0, "v_b": 6, "fc1": 7}

        names = """settled x_in0 x_in1 x_in2 x_in3 w_in0 w_in1 w_in2 rows_in mask_in gate_out gate_in y_out
            ident_ok half_ok consts stats_bn stats_ok mod_ok silu_ok film_mm film_ok silu_e silu_chain film_one
            ada_mm ada_ok gate_mm gate_ok bias_mm wvp_mm
            wvp_ok bcol_ok pbias_ok valid_ok mod32_ok selc_ok mterm_ok selbase_ok pick_ok
            a_pow a_xn a_xb a_T a_h a_Q a_K a_V a_qT a_kT a_v a_S a_max a_exp a_PT a_pT a_PV a_rden a_res
            b_pow b_xn b_xb b_T b_h b_M1 b_gelu b_M2 b_res
            c_pow c_xb c_gp c_nv c_sel c_qbv c_xc c_Tx c_h c_QK c_V c_q c_k c_v c_hiq c_hik c_lo c_Tq c_Tk c_qT c_kT
            c_S c_max c_nm c_NT c_nmT c_ST c_exp c_PV c_oT c_T2 c_rden c_on c_T3 c_onT c_pr c_at c_res c_vinit
            d_pow d_xn d_xb d_T d_h d_M1 d_gelu d_M2 d_gm d_res d_gp""".split()
        s = {n: sem(n) for n in names}

        RMS = 2 * G + 2
        LN = 2 * G + 2

        def settled(eng):
            eng.sem_inc(s["settled"], 1)

        def batch(t, b):
            return t[:, bass.ds(b, 1), :].rearrange("p a c -> p (a c)")

        block = ctx.enter_context(nc.Block())

        @block.sync
        def _(sp):
            sp.dma_start(W[:, 0:W_AT["x_end"]], weights[:, 0:W_AT["x_end"]]).then_inc(s["w_in0"], 16)
            sp.dma_start(xs[:, 0:G], x[:, 0:G]).then_inc(s["x_in0"], 16)
            sp.dma_start(R[:, :], rows.partition_broadcast(128)).then_inc(s["rows_in"], 16)
            for g in range(1, 4):
                sp.dma_start(xs[:, G * g:G * g + G], x[:, G * g:G * g + G]).then_inc(s[f"x_in{g}"], 16)
            sp.dma_start(W[:, W_AT["ada"]:W_ALL], weights[:, W_AT["ada"]:W_ALL]).then_inc(s["w_in2"], 16)
            sp.dma_start(W[:, W_AT["mlp1"]:W_AT["m_end"]], weights[:, W_AT["mlp1"]:W_AT["m_end"]]).then_inc(s["w_in1"], 16)
            sp.dma_start(mask_i[:], mask.rearrange("b n -> (b n)").partition_broadcast(128)).then_inc(s["mask_in"], 16)
            sp.dma_start(maskt_i[:], mask_t).then_inc(s["mask_in"], 16)
            sp.wait_ge(s["gate_ok"], 1)
            sp.dma_start(gates, gate_rows[:].rearrange("b g c -> b (g c)")).then_inc(s["gate_out"], 16)
            sp.wait_ge(s["gate_out"], 16)
            sp.dma_start(gate[:], gates.rearrange("b f -> (b f)").partition_broadcast(128)).then_inc(s["gate_in"], 16)
            for g in range(4):
                sp.wait_ge(s["d_res"], g + 1)
                sp.dma_start(out[:, G * g:G * g + G], xs[:, G * g:G * g + G]).then_inc(s["y_out"], 16)
            sp.wait_ge(s["y_out"], 64)

        @block.tensor
        def _(pe):
            mm = nc.tensor.matmul
            pe.wait_ge(s["w_in0"], 16)
            for j in range(4):
                ins = mm(ps[:, 7, B * j:B * j + B], w(("film1", "film2")[j // 2], C, C * (j % 2)), w("cond", B),
                         start=(j == 0), stop=True, skip_group_check=True)
            ins.then_inc(s["film_mm"], 1)
            mm(ps[:, 6, 0:C], w("vt"), w("proj"), start=True, stop=True).then_inc(s["wvp_mm"], 1)
            pe.wait_ge(s["bcol_ok"], 1)
            mm(ps[:, 5, 0:C], bcol[:], w("proj"), start=True, stop=True).then_inc(s["wvp_mm"], 1)
            pe.wait_ge(s["ident_ok"], 4)

            def transposes(dst, src, signal):
                for j in range(G):
                    ins = nc.tensor.transpose(dst[:, j], src[:, j], ident[:])
                ins.then_inc(signal, 1)

            def ada():
                pe.wait_ge(s["w_in2"], 16)
                pe.wait_ge(s["silu_ok"], 1)
                for n, j in enumerate((1, 4, 0, 3)):
                    ins = mm(ps[:, 7, B * n:B * n + B], w("ada", C, C * j), silu[:], start=(n == 0), stop=True,
                             skip_group_check=True)
                ins.then_inc(s["ada_mm"], 1)
                pe.wait_ge(s["ada_ok"], 1)
                for n, j in enumerate((2, 5)):
                    ins = mm(ps[0:B, 7, C * n:C * n + C], silu[:], w("ada", C, C * j), start=(n == 0), stop=True,
                             skip_group_check=True)
                ins.then_inc(s["gate_mm"], 1)
                pe.wait_ge(s["gate_ok"], 1)
                pe.wait_ge(s["bcol_ok"], 2)
                mm(ps[:, 7, 0:C], bcol1[:], w("proj1"), start=True, stop=True).then_inc(s["bias_mm"], 1)

            with pe.Fori(0, 2) as i:
                for u in range(2):
                    g = 2 * i + u
                    pe.wait_ge(s["a_xn"], g + 1)
                    transposes(bank(0), xn[u], s["a_T"])
                    pe.wait_ge(s["a_h"], g + 1)
                    mm(ps[:, 1, :], w("q"), hT[u][:], start=True, stop=True).then_inc(s["a_Q"], 1)
                    mm(ps[:, 2, :], w("k"), hT[u][:], start=True, stop=True).then_inc(s["a_K"], 1)
                    pe.wait_ge(s["wvp_ok"], 1)
                    for j in range(G):
                        ins = mm(bank(3)[:, j], hT[u][:, j], wvp[:], start=True, stop=True, skip_group_check=True)
                    ins.then_inc(s["a_V"], 1)
                    pe.wait_ge(s["a_qT"], g + 1)
                    pe.wait_ge(s["a_kT"], g + 1)
                    pe.wait_ge(s["a_v"], g + 1)
                    for j in range(G):
                        ins = mm(bank(4 + 3 * u)[:, j], qT[u][:, j], kT[u][:, j], start=True, stop=True, skip_group_check=True)
                    ins.then_inc(s["a_S"], 1)
                for u in range(2):
                    g = 2 * i + u
                    pe.wait_ge(s["a_exp"], G * (g + 1))
                    transposes(bank(5), p0[u], s["a_PT"])
                    pe.wait_ge(s["a_pT"], g + 1)
                    for j in range(G):
                        ins = mm(bank(6 - 3 * u)[:, j], pT0[u][:, j], v0[u][:, j], start=True, stop=True, skip_group_check=True)
                    ins.then_inc(s["a_PV"], 1)
            ada()

            def mlp(p, w1, w2):
                with pe.Fori(0, 2) as i:
                    for u in range(2):
                        g = 2 * i + u
                        pe.wait_ge(s[p + "xn"], g + 1)
                        transposes(bank(7 * u), xn[u], s[p + "T"])
                    for u in range(2):
                        g = 2 * i + u
                        pe.wait_ge(s[p + "h"], g + 1)
                        for f in range(FC):
                            if u:
                                pe.wait_ge(s[p + "gelu"], FC * (g - 1) + f + 1)
                            mm(ps[:, 1 + f, :], w(w1, C, C * f), hT[u][:], start=True, stop=True).then_inc(s[p + "M1"], 1)
                    for u in range(2):
                        g = 2 * i + u
                        pe.wait_ge(s[p + "gelu"], FC * (g + 1))
                        for j in range(G):
                            for f in range(FC):
                                ins = mm(bank(5 + u)[:, j], hid[u][:, f, j], w(w2, C, C * f),
                                         start=(f == 0), stop=(f == FC - 1), skip_group_check=True)
                        ins.then_inc(s[p + "M2"], 1)

            pe.wait_ge(s["w_in1"], 16)
            pe.wait_ge(s["a_res"], 16)
            pe.wait_ge(s["pbias_ok"], 1)
            mlp("b_", "mlp1", "mlp2")

            def front_a(b, u):
                pe.wait_ge(s["c_xc"], b + 1)
                nc.tensor.transpose(ps[:, 6, 0:N], xc[u][:], ident[:]).then_inc(s["c_Tx"], 1)

            def front_b(b, u):
                pe.wait_ge(s["c_h"], b + 1)
                mm(ps[:, 4, 0:2 * C], hc[u][:], w("qkv", 2 * C), start=True, stop=True).then_inc(s["c_QK"], 1)
                mm(ps[:, 6, 0:C], hc[u][:], w("qkv", C, 2 * C), start=True, stop=True).then_inc(s["c_V"], 1)

            def front_c(b, u):
                pe.wait_ge(s["c_v"], b + 1)
                pe.wait_ge(s["c_lo"], 2 * b + 1)
                q = qkx[u][:].rearrange("n q (t r) s d -> n q t (r s d)", t=4)
                for t in range(4):
                    ins = nc.tensor.transpose(bank(6)[:, t], q[:, 0, t], ident[:])
                ins.then_inc(s["c_Tq"], 1)
                pe.wait_ge(s["c_lo"], 2 * b + 2)
                for t in range(4):
                    ins = nc.tensor.transpose(bank(7)[:, t], q[:, 1, t], ident[:])
                ins.then_inc(s["c_Tk"], 1)

            def scores(b, u, e, first):
                if e == 0:
                    pe.wait_ge(s["c_qT"], b + 1)
                    pe.wait_ge(s["c_kT"], b + 1)
                    pe.wait_ge(s["c_sel"], b + 1)
                for r in (2 * e, 2 * e + 1):
                    q = slice(32 * r, 32 * r + 32)
                    mm(ps[:, r, :], pick_mask[q, :], sel[u][q], start=True, stop=False, skip_group_check=True)
                for t in range(4):
                    for r in (2 * e, 2 * e + 1):
                        q = slice(32 * r, 32 * r + 32)
                        ins = mm(bank(r)[:, t], qxT[u][q, t], kxT[u][q, t], start=False, stop=True, skip_group_check=True)
                ins.then_inc(s["c_S"], 1)

            def scores_t(b, u, e):
                for t in range(4):
                    for r in (2 * e, 2 * e + 1):
                        q = slice(32 * r, 32 * r + 32)
                        mm(bank(r)[:, t], sel[u][q, t], nmT[u][q, :], start=(t == 0), stop=False, skip_group_check=True)
                for t in range(4):
                    for r in (2 * e, 2 * e + 1):
                        q = slice(32 * r, 32 * r + 32)
                        ins = mm(bank(r)[:, t], kxT[u][q, t], qxT[u][q, t], start=False, stop=True, skip_group_check=True)
                ins.then_inc(s["c_ST"], 1)

            def weighted(b, u, e):
                pe.wait_ge(s["c_exp"], 2 * b + e + 1)
                v = vx[u][:].rearrange("n (e t s c) -> n e t s c", e=2, t=4, s=2)
                for s2 in range(2):
                    for t in range(4):
                        ins = mm(ps[32 * t:32 * t + 32, 5, N * e:N * e + N], v[:, e, t, s2], pT[u][:, 2 * e + s2, t],
                                 start=(s2 == 0), stop=(s2 == 1), skip_group_check=True)
                ins.then_inc(s["c_PV"], 1)

            def back_a(b, u):
                pe.wait_ge(s["c_oT"], b + 1)
                for e in range(2):
                    ins = nc.tensor.transpose(ps[:, 4, 128 * e:128 * e + 128], oT[u][:, e], ident[:])
                ins.then_inc(s["c_T2"], 1)

            def back_b(b, u):
                pe.wait_ge(s["c_on"], b + 1)
                nc.tensor.transpose(ps[:, 5, 0:N], on[u][:].rearrange("n h d -> n (h d)"), ident[:]).then_inc(s["c_T3"], 1)

            def back_c(b, u):
                pe.wait_ge(s["c_onT"], b + 1)
                mm(ps[:, 7, 0:C], onT[u][:], w("proj1"), start=True, stop=True).then_inc(s["c_pr"], 1)

            def step(b, u, first=False, last=False):
                scores(b, u, 0, first)
                if not first:
                    back_a(b - 1, 1 - u)
                scores(b, u, 1, first)
                if not first:
                    back_b(b - 1, 1 - u)
                if not last:
                    front_a(b + 1, 1 - u)
                if not first:
                    back_c(b - 1, 1 - u)
                if not last:
                    front_b(b + 1, 1 - u)
                pe.wait_ge(s["c_nm"], 4 * b + 4)
                nc.tensor.transpose(ps[:, 5, 0:N // 2].bitcast(BF16), nm[u][:].rearrange("n r k -> n (r k)"),
                                    identb[:]).then_inc(s["c_NT"], 1)
                pe.wait_ge(s["c_nmT"], b + 1)
                scores_t(b, u, 0)
                scores_t(b, u, 1)
                if not last:
                    if not first:
                        pe.wait_ge(s["c_at"], b)
                    front_c(b + 1, 1 - u)
                if first:
                    pe.wait_ge(s["c_vinit"], 8)
                pe.wait_ge(s["c_v"], b + 1)
                weighted(b, u, 0)
                weighted(b, u, 1)

            pe.wait_ge(s["pick_ok"], 1)
            pe.wait_ge(s["b_res"], 4)
            front_a(0, 0)
            front_b(0, 0)
            front_c(0, 0)
            step(0, 0, first=True)
            with pe.Fori(0, 7) as i:
                step(2 * i + 1, 1)
                step(2 * i + 2, 0)
            step(B - 1, 1, last=True)
            back_a(B - 1, 1)
            back_b(B - 1, 1)
            back_c(B - 1, 1)

            pe.wait_ge(s["c_at"], B)
            mlp("d_", "fc1", "fc2")

        @block.scalar
        def _(act):
            a = nc.scalar.activation
            act.wait_ge(s["w_in0"], 16)
            a(cond_e[:], w("cond", B), ACT.Exp, scale=-1.0).then_inc(s["silu_e"], 1)
            act.wait_ge(s["wvp_mm"], 1)
            a(wvp[:], ps[:, 6, 0:C], ACT.Copy).then_inc(s["wvp_ok"], 1)

            def affine(dst, src, k, b, signal):
                for j in range(G):
                    ins = a(dst[:, j], src[:, j], ACT.Identity, bias=shift[:, k, bass.ds(b + j, 1)],
                            scale=scale[:, k, bass.ds(b + j, 1)])
                ins.then_inc(signal, 1)

            act.wait_ge(s["film_ok"], 2)
            with act.Fori(0, 2) as i:
                for u in range(2):
                    g = 2 * i + u
                    act.wait_ge(s["a_T"], g + 1)
                    settled(act)
                    affine(hT[u], bank(0), 0, G * g, s["a_h"])
                    act.wait_ge(s["a_K"], g + 1)
                    a(kT[u][:], bank(2), ACT.Identity, bias=col("cols0", COL["k_b"])).then_inc(s["a_kT"], 1)
                for u in range(2):
                    g = 2 * i + u
                    act.wait_ge(s["a_max"], g + 1)
                    for j in range(G):
                        a(p0[u][:, j], bank(4 + 3 * u)[:, j], ACT.Exp, bias=amax[:, u, j:j + 1],
                          accum_out=aden[:, u, j:j + 1]).then_inc(s["a_exp"], 1)

            def mlp(p, k, func, bcols, bat):
                with act.Fori(0, 2) as i:
                    for u in range(2):
                        g = 2 * i + u
                        for f in range(FC):
                            act.wait_ge(s[p + "M1"], FC * g + f + 1)
                            a(hid[u][:, f], bank(1 + f), func, bias=col(bcols, bat + f)).then_inc(s[p + "gelu"], 1)

            mlp("b_", 1, ACT.Gelu, "cols0", COL["mlp_b1"])

            def front_a(b, u):
                act.wait_ge(s["c_Tx"], b + 1)
                act.wait_ge(s["ada_ok"], 1)
                a(hc[u][:], ps[:, 6, 0:N], ACT.Identity, bias=shift[:, 2, bass.ds(b, 1)],
                  scale=scale[:, 2, bass.ds(b, 1)]).then_inc(s["c_h"], 1)

            def front_b(b, u):
                act.wait_ge(s["c_q"], b + 1)
                a(qkx[u][:, 0, :, 0:2].bitcast(F32R), qk[u][:, 0].unsqueeze(2).broadcast_to((N, H, 2, HD)),
                  ACT.Copy).then_inc(s["c_hiq"], 1)
                act.wait_ge(s["c_k"], b + 1)
                a(qkx[u][:, 1, :, 0:4:2].bitcast(F32R), qk[u][:, 1].unsqueeze(2).broadcast_to((N, H, 2, HD)),
                  ACT.Copy).then_inc(s["c_hik"], 1)

            def v_slots(u):
                v = vx[u][:].rearrange("n (a z) -> n a z", z=64)
                return [v[:, :, 48 * k:48 * k + 16] for k in range(2)]

            def front_v(b, u, first=False):
                act.wait_ge(s["c_V"], b + 1)
                v = ps[:, 6, 0:C].rearrange("n (a k d) -> n a k d", k=2, d=HD)
                for k in range(2):
                    ins = a(v_slots(u)[k][:, :, 0:HD], v[:, :, k], ACT.Copy)
                    if k:
                        ins.then_inc(s["c_v"], 1)

            def front_c(b, u):
                act.wait_ge(s["c_Tq"], b + 1)
                a(qxT[u][:], bank(6), ACT.Copy).then_inc(s["c_qT"], 1)
                act.wait_ge(s["c_Tk"], b + 1)
                a(kxT[u][:], bank(7), ACT.Copy).then_inc(s["c_kT"], 1)

            def step(b, u, first=False, last=False):
                if not first:
                    act.wait_ge(s["c_T3"], b)
                    a(onT[1 - u][:], ps[:, 5, 0:N], ACT.Copy).then_inc(s["c_onT"], 1)
                if not last:
                    front_a(b + 1, 1 - u)
                    front_v(b + 1, 1 - u)
                    front_b(b + 1, 1 - u)
                for e in range(2):
                    act.wait_ge(s["c_ST"], 2 * b + e + 1)
                    a(pT[u][:, 2 * e:2 * e + 2], ps[:, 2 * e:2 * e + 2, :].rearrange("n r (t q) -> n r t q", t=4),
                      ACT.Exp, scale=HD ** -0.5).then_inc(s["c_exp"], 1)
                if not last:
                    front_c(b + 1, 1 - u)
                act.wait_ge(s["c_PV"], 2 * b + 2)
                a(oT[u][:], ps[:, 5, 0:2 * N].rearrange("p (e n) -> p e n", e=2), ACT.Copy).then_inc(s["c_oT"], 1)

            act.wait_ge(s["c_vinit"], 4)
            front_a(0, 0)
            front_v(0, 0)
            front_b(0, 0)
            front_c(0, 0)
            step(0, 0, first=True)
            with act.Fori(0, 7) as i:
                step(2 * i + 1, 1)
                step(2 * i + 2, 0)
            step(B - 1, 1, last=True)
            act.wait_ge(s["c_T3"], B)
            a(onT[1][:], ps[:, 5, 0:N], ACT.Copy).then_inc(s["c_onT"], 1)

            mlp("d_", 3, ACT.Gelu_apprx_tanh, "cols1", COL1["fc1"])

        @block.vector
        def _(dve):
            v = nc.vector
            v.memset(half[:], -0.5).then_inc(s["half_ok"], 1)

            def group_stats(k, g, base, rms):
                b = G * g
                for j in range(G):
                    v.bn_stats(bn[:, j], xs[:, bass.ds(b + j, 1), :].rearrange("p a c -> p (a c)")).then_inc(s["stats_bn"], 1)
                dve.wait_ge(s["stats_bn"], base + G)
                settled(dve)
                for j in range(G):
                    v.bn_aggr(agg[:, j], bn[:, j]).then_inc(s["stats_bn"], 1)
                ve = var_eps[:, k, bass.ds(b, G)]
                dve.wait_ge(s["stats_bn"], base + 2 * G)
                settled(dve)
                if rms:
                    v.tensor_tensor(mean_sq[:], agg[:, :, 0], agg[:, :, 0], ALU.mult).then_inc(s["stats_bn"], 1)
                    dve.wait_ge(s["stats_bn"], base + 2 * G + 1)
                    settled(dve)
                    v.scalar_tensor_tensor(out=ve, in0=agg[:, :, 1], scalar=EPS, in1=mean_sq[:], op0=ALU.add, op1=ALU.add)\
                        .then_inc(s["stats_bn"], 1)
                else:
                    v.tensor_copy(mean[:, k - 2, bass.ds(b, G)], agg[:, :, 0]).then_inc(s["stats_bn"], 1)
                    v.tensor_scalar(ve, agg[:, :, 1], EPS, None, ALU.add).then_inc(s["stats_bn"], 1)

            for g in range(4):
                dve.wait_ge(s[f"x_in{g}"], 16)
                group_stats(0, g, RMS * g, True)
                if g == 0:
                    dve.wait_ge(s["film_mm"], 1)
                    for k, c in enumerate(("film1", "film2")):
                        v.tensor_scalar(scale[:, k, :], ps[:, 7, 2 * B * k:2 * B * k + B], col("cols0", COL[c]), 1.0,
                                        ALU.add, ALU.add).then_inc(s["film_one"], 1)
                        v.tensor_scalar(shift[:, k, :], ps[:, 7, 2 * B * k + B:2 * B * k + 2 * B],
                                        col("cols0", COL[c] + 1), None, ALU.add).then_inc(s["film_one"], 1)
                    dve.wait_ge(s["film_one"], 4)
                    for k, n in enumerate(("n1", "n2")):
                        v.tensor_scalar(scale[:, k, :], scale[:, k, :], col("cols0", COL[n]), None, ALU.mult)\
                            .then_inc(s["film_ok"], 1)
                if g == 1:
                    dve.wait_ge(s["wvp_mm"], 2)
                    dve.wait_ge(s["rows_in"], 16)
                    v.tensor_tensor(bias_a[:], ps[:, 5, 0:C], row("proj_b"), ALU.add).then_inc(s["wvp_ok"], 1)
            dve.wait_ge(s["silu_e"], 1)
            v.tensor_scalar(cond_s[:], cond_e[:], 1.0, None, ALU.add).then_inc(s["silu_chain"], 1)
            dve.wait_ge(s["silu_chain"], 1)
            v.reciprocal(cond_r[:], cond_s[:]).then_inc(s["silu_chain"], 1)
            dve.wait_ge(s["silu_chain"], 2)
            v.tensor_tensor(silu[:], w("cond", B), cond_r[:], ALU.mult).then_inc(s["silu_ok"], 1)

            def res_a(i, u):
                g = 2 * i + u
                dve.wait_ge(s["a_exp"], G * (g + 1))
                v.reciprocal(arden[:, u, :], aden[:, u, :]).then_inc(s["a_rden"], 1)
                dve.wait_ge(s["a_rden"], g + 1)
                dve.wait_ge(s["a_xb"], g + 1)
                dve.wait_ge(s["a_PV"], g + 1)
                settled(dve)
                for j in range(G):
                    b = G * g + j
                    v.scalar_tensor_tensor(out=xs[:, bass.ds(b, 1), :].rearrange("p a c -> p (a c)"), in0=bank(6 - 3 * u)[:, j],
                                           scalar=arden[:, u, j:j + 1],
                                           in1=xb[:, bass.ds(b, 1), :].rearrange("p a c -> p (a c)"),
                                           op0=ALU.mult, op1=ALU.add).then_inc(s["a_res"], 1)

            with dve.Fori(0, 2) as i:
                for u in range(2):
                    g = 2 * i + u
                    dve.wait_ge(s["a_pow"], g + 1)
                    settled(dve)
                    for j in range(G):
                        b = G * g + j
                        ins = v.tensor_scalar(xn[u][:, j], batch(xs, b), rstd[:, 0, bass.ds(b, 1)], None, ALU.mult)
                    ins.then_inc(s["a_xn"], 1)
                for u in range(2):
                    g = 2 * i + u
                    dve.wait_ge(s["a_Q"], g + 1)
                    v.tensor_scalar(qT[u][:], bank(1), col("cols0", COL["q_b"]), C ** -0.5, ALU.add, ALU.mult)\
                        .then_inc(s["a_qT"], 1)
                    dve.wait_ge(s["a_V"], g + 1)
                    v.tensor_copy(v0[u][:], bank(3)).then_inc(s["a_v"], 1)
                    dve.wait_ge(s["a_S"], g + 1)
                    v.tensor_reduce(amax[:, u, :], bank(4 + 3 * u), AX.X, ALU.max, negate=True).then_inc(s["a_max"], 1)
                for u in range(2):
                    g = 2 * i + u
                    dve.wait_ge(s["a_PT"], g + 1)
                    v.tensor_copy(pT0[u][:], bank(5)).then_inc(s["a_pT"], 1)
                    res_a(i, u)
                    dve.wait_ge(s["a_res"], G * (g + 1))
                    settled(dve)
                    group_stats(1, g, RMS * (4 + g), True)

            def mlp(p, k, base):
                with dve.Fori(0, 2) as i:
                    for u in range(2):
                        g = 2 * i + u
                        dve.wait_ge(s[p + "pow"], g + 1)
                        settled(dve)
                        for j in range(G):
                            b = G * g + j
                            if p == "b_":
                                ins = v.tensor_scalar(xn[u][:, j], batch(xs, b), rstd[:, k, bass.ds(b, 1)], None, ALU.mult)
                            else:
                                ins = v.tensor_scalar(xn[u][:, j], batch(xs, b),
                                                      mean[:, k - 2, bass.ds(b, 1)],
                                                      rstd[:, k, bass.ds(b, 1)], ALU.subtract, ALU.mult)
                        ins.then_inc(s[p + "xn"], 1)
                    for u in range(2):
                        g = 2 * i + u
                        dve.wait_ge(s[p + "T"], g + 1)
                        settled(dve)
                        for j in range(G):
                            b = G * g + j
                            ins = v.tensor_scalar(hT[u][:, j], bank(7 * u)[:, j], scale[:, k, bass.ds(b, 1)],
                                                  shift[:, k, bass.ds(b, 1)], ALU.mult, ALU.add)
                        ins.then_inc(s[p + "h"], 1)
                    for u in range(2):
                        g = 2 * i + u
                        b = G * g
                        dve.wait_ge(s[p + "M2"], g + 1)
                        dve.wait_ge(s[p + "xb"], g + 1)
                        settled(dve)
                        if p == "b_":
                            v.tensor_tensor(xs[:, bass.ds(b, G), :], bank(5 + u), xb[:, bass.ds(b, G), :], ALU.add)\
                                .then_inc(s["b_res"], 1)
                            dve.wait_ge(s["b_res"], g + 1)
                            settled(dve)
                            group_stats(2, g, base + LN * g, False)
                        else:
                            v.tensor_tensor(gmul[u][:], bank(5 + u), gate[:, bass.ds(b, G), 1, :], ALU.mult)\
                                .then_inc(s["d_gm"], 1)
                            dve.wait_ge(s["d_gm"], g + 1)
                            settled(dve)
                            v.tensor_tensor(xs[:, bass.ds(b, G), :], gmul[u][:], xb[:, bass.ds(b, G), :], ALU.add)\
                                .then_inc(s["d_res"], 1)

            dve.wait_ge(s["ada_mm"], 1)
            for n, j in enumerate((1, 4, 0, 3)):
                dst = scale[:, 2 + n, :] if n < 2 else shift[:, n, :]
                ins = v.tensor_scalar(dst, ps[:, 7, B * n:B * n + B], col("cols1", COL1["ada"] + j),
                                      1.0 if n < 2 else 0.0, ALU.add, ALU.add)
            ins.then_inc(s["ada_ok"], 1)
            dve.wait_ge(s["gate_mm"], 1)
            v.tensor_tensor(gate_rows[:].rearrange("b g c -> b (g c)"), ps[0:B, 7, 0:2 * C], row("gate_b", 2 * C)[0:B, :],
                            ALU.add).then_inc(s["gate_ok"], 1)
            dve.wait_ge(s["bias_mm"], 1)
            v.tensor_tensor(pbias1[:], ps[:, 7, 0:C], row("proj1_b"), ALU.add).then_inc(s["pbias_ok"], 1)
            dve.wait_ge(s["ident_ok"], 4)
            dve.wait_ge(s["mask_in"], 32)
            v.tensor_copy(valid[:], maskt_i[:]).then_inc(s["valid_ok"], 1)
            v.tensor_reduce(mod32[:], ident[:].rearrange("p (r k) -> p k r", r=4), AX.X, ALU.add).then_inc(s["mod32_ok"], 1)
            dve.wait_ge(s["mod32_ok"], 1)
            v.tensor_reduce(sel_f[:], mod32[:, 0:12].rearrange("p (k t) -> p t k", t=4), AX.X, ALU.add)
            v.tensor_scalar(row_amp[:], mod32[:, MROW:MROW + 1], -MASKED, None, ALU.mult)
            v.tensor_scalar(row_neg[:], mod32[:, MROW:MROW + 1], MASKED, None, ALU.mult).then_inc(s["selc_ok"], 1)

            mlp("b_", 1, RMS * 8)

            def front(b, u):
                dve.wait_ge(s["c_QK"], b + 1)
                dve.wait_ge(s["c_qbv"], b + 1)
                settled(dve)
                v.scalar_tensor_tensor(out=qk[u][:, 0].rearrange("n h d -> n (h d)"), in0=ps[:, 4, 0:C],
                                       scalar=valid[:, bass.ds(b, 1)], in1=qbv[u][:], op0=ALU.mult, op1=ALU.add)\
                    .then_inc(s["c_q"], 1)
                v.tensor_tensor(qk[u][:, 1].rearrange("n h d -> n (h d)"), ps[:, 4, C:2 * C], row("qk_b", C, C), ALU.add)\
                    .then_inc(s["c_k"], 1)

            def maxima(b, u, e):
                dve.wait_ge(s["c_S"], 2 * b + e + 1)
                v.tensor_reduce(nmax[u][:, 8 * e:8 * e + 8],
                                ps[:, 2 * e:2 * e + 2, :].rearrange("n r (t k) -> n (r t) k", t=4), AX.X, ALU.max,
                                negate=True).then_inc(s["c_max"], 1)

            def split_max(b, u):
                m = nmax[u][:].rearrange("n (r t) -> n r t", r=4)
                rest = mrest[u][:].rearrange("n (r t) -> n r t", r=4)
                dve.wait_ge(s["c_max"], 2 * b + 2)
                settled(dve)
                v.tensor_scalar(nm[u][:, :, 0:4], m, valid[:, bass.ds(b, 1)], None, ALU.mult).then_inc(s["c_nm"], 1)
                dve.wait_ge(s["c_nm"], 4 * b + 1)
                settled(dve)
                v.scalar_tensor_tensor(out=rest, in0=m, scalar=valid[:, bass.ds(b, 1)], in1=nm[u][:, :, 0:4],
                                       op0=ALU.mult, op1=ALU.subtract).then_inc(s["c_nm"], 1)
                dve.wait_ge(s["c_nm"], 4 * b + 2)
                v.tensor_copy(nm[u][:, :, 4:8], rest).then_inc(s["c_nm"], 1)
                dve.wait_ge(s["c_nm"], 4 * b + 3)
                v.tensor_tensor(nm[u][:, :, 8:12], rest, nm[u][:, :, 4:8], ALU.subtract).then_inc(s["c_nm"], 1)
                dve.wait_ge(s["c_NT"], b + 1)
                v.tensor_copy(nmT[u][:], ps[:, 5, 0:N // 2].bitcast(BF16)).then_inc(s["c_nmT"], 1)

            def normalise(b, u):
                o = ps[:, 4, 0:256].rearrange("n (h z) -> n h z", z=16)
                dve.wait_ge(s["c_T2"], b + 1)
                v.reciprocal(rden[u][:], o[:, :, HD]).then_inc(s["c_rden"], 1)
                dve.wait_ge(s["c_rden"], b + 1)
                v.tensor_tensor(on[u][:], o[:, :, 0:HD], rden[u][:].unsqueeze(2).broadcast_to((N, 16, HD)), ALU.mult)\
                    .then_inc(s["c_on"], 1)

            def gated(b, u):
                dve.wait_ge(s["c_pr"], b + 1)
                dve.wait_ge(s["gate_in"], 16)
                v.tensor_tensor(attn[u][:], ps[:, 7, 0:C],
                                gate[:, bass.ds(b, 1), 0, :].rearrange("p a c -> p (a c)"), ALU.mult)\
                    .then_inc(s["c_at"], 1)

            def norm(b, u):
                if not isinstance(b, int) or b >= 2:
                    dve.wait_ge(s["c_Tx"], b - 1)
                settled(dve)
                v.tensor_scalar(xc[u][:], batch(xs, b), mean[:, 0, bass.ds(b, 1)],
                                rstd[:, 2, bass.ds(b, 1)], ALU.subtract, ALU.mult).then_inc(s["c_xc"], 1)

            def step(b, u, first=False, last=False):
                if not last:
                    norm(b + 1, 1 - u)
                maxima(b, u, 0)
                if not first:
                    normalise(b - 1, 1 - u)
                maxima(b, u, 1)
                split_max(b, u)
                if not first:
                    gated(b - 1, 1 - u)
                if not last:
                    front(b + 1, 1 - u)

            dve.wait_ge(s["c_pow"], 4)
            norm(0, 0)
            front(0, 0)
            step(0, 0, first=True)
            with dve.Fori(0, 7) as i:
                step(2 * i + 1, 1)
                step(2 * i + 2, 0)
            step(B - 1, 1, last=True)
            normalise(B - 1, 1)
            dve.wait_ge(s["c_res"], B - 2)
            gated(B - 1, 1)

            for g in range(4):
                dve.wait_ge(s["c_res"], G * (g + 1))
                group_stats(3, g, RMS * 8 + LN * 4 + LN * g, False)
            mlp("d_", 3, 0)

        @block.gpsimd
        def _(pool):
            p = nc.gpsimd
            for m in (ident, identb):
                p.memset(m[:], 0.0).then_inc(s["ident_ok"], 1)
            pool.wait_ge(s["ident_ok"], 2)
            for m in (ident, identb):
                p.affine_select(out=m[:], in_=m[:], compare_op=ALU.not_equal, fill=1.0, base=0,
                                pattern=[[-1, 128]], channel_multiplier=1).then_inc(s["ident_ok"], 1)
            pool.wait_ge(s["ident_ok"], 4)
            pool.wait_ge(s["w_in0"], 16)
            p.tensor_scalar(bcol[:], ident[:], 0.0, col("cols0", COL["v_b"]), ALU.mult, ALU.add).then_inc(s["bcol_ok"], 1)

            def root(k, g, need, signal):
                pool.wait_ge(s["stats_bn"], need)
                settled(pool)
                p.tensor_tensor(rstd[:, k, bass.ds(G * g, G)], var_eps[:, k, bass.ds(G * g, G)],
                                half[:, 0:G], ALU.pow).then_inc(signal, 1)

            def bias_add(g, bias, signal):
                b = G * g
                p.tensor_tensor(xb[:, bass.ds(b, G), :], xs[:, bass.ds(b, G), :],
                                bias.unsqueeze(1).broadcast_to((N, G, C)), ALU.add).then_inc(signal, 1)

            with pool.Fori(0, 2) as i:
                for u in range(2):
                    g = 2 * i + u
                    root(0, g, RMS * g + RMS, s["a_pow"])
                    pool.wait_ge(s["wvp_ok"], 2)
                    bias_add(g, bias_a[:], s["a_xb"])

            pool.wait_ge(s["w_in2"], 16)
            p.tensor_scalar(bcol1[:], ident[:], 0.0, col("cols1", COL1["v_b"]), ALU.mult, ALU.add).then_inc(s["bcol_ok"], 1)

            with pool.Fori(0, 2) as i:
                for u in range(2):
                    g = 2 * i + u
                    root(1, g, RMS * (4 + g) + RMS, s["b_pow"])
                for u in range(2):
                    bias_add(2 * i + u, row("mlp_b2"), s["b_xb"])

            pool.wait_ge(s["selc_ok"], 1)
            p.tensor_scalar(mask_term[:].rearrange("p b n -> p (b n)"), mask_i[:].rearrange("p b n -> p (b n)"),
                            row_amp[:, 0:1], row_neg[:, 0:1], ALU.mult, ALU.add).then_inc(s["mterm_ok"], 1)
            p.tensor_copy(sel_base[:], sel_f[:].unsqueeze(2).broadcast_to((128, 4, N))).then_inc(s["selbase_ok"], 1)
            p.tensor_copy(pick_mask[:], mod32[:, MROW:MROW + 1].broadcast_to((128, N))).then_inc(s["pick_ok"], 1)
            for u in range(2):
                p.memset(vx[u][:], 0.0).then_inc(s["c_vinit"], 1)
                p.memset(nm[u][:], 0.0).then_inc(s["c_vinit"], 1)
            pool.wait_ge(s["c_vinit"], 4)
            for u in range(2):
                for k in range(2):
                    z = vx[u][:].rearrange("n (a z) -> n a z", z=64)[:, :, 48 * k + HD:48 * k + HD + 1]
                    p.memset(z, 1.0).then_inc(s["c_vinit"], 1)

            def prepare(b, u):
                if not isinstance(b, int) or b >= 2:
                    pool.wait_ge(s["c_ST"], 2 * b - 2)
                else:
                    pool.wait_ge(s["selbase_ok"], 1)
                settled(pool)
                p.tensor_tensor(sel[u][:], sel_base[:], mask_term[:, bass.ds(b, 1), :].broadcast_to((128, 4, N)), ALU.add)\
                    .then_inc(s["c_sel"], 1)
                p.tensor_copy(nm[u][:, :, MROW], valid[:, bass.ds(b, 1)].broadcast_to((N, 4))).then_inc(s["c_nv"], 1)
                p.tensor_tensor(qbv[u][:], row("qk_b"), valid[:, bass.ds(b, 1)].broadcast_to((N, C)), ALU.mult)\
                    .then_inc(s["c_qbv"], 1)
                p.tensor_tensor(gtmp[:, u], gate[:, bass.ds(b, 1), 0, :].rearrange("p a c -> p (a c)"), pbias1[:], ALU.mult)\
                    .then_inc(s["c_gp"], 1)
                pool.wait_ge(s["c_gp"], b + 1)
                settled(pool)
                p.tensor_tensor(batch(xb, b), batch(xs, b), gtmp[:, u], ALU.add).then_inc(s["c_xb"], 1)

            def lower(b, u):
                for n, (hi, lo, signal) in enumerate(((slice(0, 2), slice(2, 4), "c_hiq"), (slice(0, 4, 2), slice(1, 4, 2), "c_hik"))):
                    pool.wait_ge(s[signal], b + 1)
                    x_ = qk[u][:, n].unsqueeze(2).broadcast_to((N, H, 2, HD))
                    p.tensor_tensor(qkx[u][:, n, :, lo].bitcast(F32R), x_, qkx[u][:, n, :, hi], ALU.subtract)\
                        .then_inc(s["c_lo"], 1)

            def residual(b, u):
                pool.wait_ge(s["c_at"], b + 1)
                pool.wait_ge(s["c_xb"], b + 1)
                settled(pool)
                p.tensor_tensor(batch(xs, b), attn[u][:], batch(xb, b), ALU.add).then_inc(s["c_res"], 1)

            for g in range(4):
                root(2, g, RMS * 8 + LN * g + LN, s["c_pow"])
            pool.wait_ge(s["mterm_ok"], 1)
            pool.wait_ge(s["gate_in"], 16)
            pool.wait_ge(s["pbias_ok"], 1)
            pool.wait_ge(s["valid_ok"], 1)
            pool.wait_ge(s["c_vinit"], 8)
            pool.wait_ge(s["b_res"], 4)
            prepare(0, 0)
            lower(0, 0)

            def step(b, u, first=False, last=False):
                if not last:
                    prepare(b + 1, 1 - u)
                    lower(b + 1, 1 - u)
                if not first:
                    residual(b - 1, 1 - u)

            step(0, 0, first=True)
            with pool.Fori(0, 7) as i:
                step(2 * i + 1, 1)
                step(2 * i + 2, 0)
            step(B - 1, 1, last=True)
            residual(B - 1, 1)

            for g in range(4):
                root(3, g, RMS * 8 + LN * 4 + LN * g + LN, s["d_pow"])
            with pool.Fori(0, 4) as g:
                b = G * g
                p.tensor_tensor(gtmp[:], gate[:, bass.ds(b, G), 1, :], row("fc2_b").unsqueeze(1).broadcast_to((N, G, C)),
                                ALU.mult).then_inc(s["d_gp"], 1)
                pool.wait_ge(s["d_gp"], g + 1)
                settled(pool)
                p.tensor_tensor(xb[:, bass.ds(b, G), :], xs[:, bass.ds(b, G), :], gtmp[:], ALU.add).then_inc(s["d_xb"], 1)
                pool.wait_ge(s["d_xb"], g + 1)


def kernel(**inputs):
    import numpy as np
    import concourse.bacc as bacc
    from concourse.bass_utils import run_bass_kernel_spmd

    a = {k: np.asarray(v) for k, v in inputs.items()}
    l0 = {k[8:]: v for k, v in a.items() if k.startswith("L0_cond_")}
    l1 = {k[8:]: v for k, v in a.items() if k.startswith("L1_cond_")}

    def columns(*vectors):
        cols = np.concatenate([v.reshape(-1, 128) for v in vectors]).T
        return np.concatenate([cols, np.zeros((128, 16 - cols.shape[1]), np.float32)], axis=1)

    order = np.arange(C).reshape(4, 2, 2, HD).transpose(1, 0, 2, 3).reshape(-1)
    qkv = l1["qkv_w"].T
    packed = {
        "cond": a["cond_1024"].T, "film1": l0["film1_w"], "film2": l0["film2_w"],
        "cols0": columns(l0["q_b"], l0["k_b"], l0["v_b"], l0["norm1_w"], l0["norm2_w"], l0["film1_b"],
                         l0["film2_b"], l0["mlp_b1"]),
        "q": l0["q_w"], "k": l0["k_w"], "vt": l0["v_w"].T, "proj": l0["proj_w"], "mlp1": l0["mlp_w1"],
        "mlp2": l0["mlp_w2"].reshape(FC, 128, C).transpose(1, 0, 2).reshape(128, F),
        "ada": l1["ada_w"].T,
        "cols1": columns(l1["ada_b"], l1["qkv_b"][2 * C:][order], l1["fc1_b"]),
        "qkv": np.concatenate([qkv[:, :2 * C], qkv[:, 2 * C:][:, order]], axis=1),
        "proj1": l1["proj_w"].T[order], "fc1": l1["fc1_w"].T,
        "fc2": l1["fc2_w"].T.reshape(FC, 128, C).transpose(1, 0, 2).reshape(128, F),
    }
    ada_b = l1["ada_b"].reshape(6, C)
    in_map = {
        "x": np.ascontiguousarray(a["x"].transpose(1, 0, 2)),
        "weights": np.ascontiguousarray(np.concatenate([packed[n] for n, size in _W if size], axis=1)),
        "rows": np.concatenate([l0["proj_b"], l0["mlp_b2"], l1["qkv_b"][:2 * C], l1["proj_b"], l1["fc2_b"],
                                ada_b[2], ada_b[5]]),
        "mask": a["mask_BxS_bk1"].astype(np.int32),
        "mask_t": np.ascontiguousarray(a["mask_BxS_bk1"].T).astype(np.int32),
    }
    nc = bacc.Bacc("TRN2", target_bir_lowering=False, num_devices=1)
    aps = [nc.dram_tensor(n, v.shape, mybir.dt.from_np(v.dtype), kind="ExternalInput").ap() for n, v in in_map.items()]
    gates = nc.dram_tensor("gates", (B, 2 * C), F32, kind="Internal").ap()
    out = nc.dram_tensor("out", (N, B, C), F32, kind="ExternalOutput").ap()
    build(nc, *aps, gates, out)
    result = run_bass_kernel_spmd(nc, [in_map], core_ids=[0])
    return np.ascontiguousarray(result.results[0]["out"].transpose(1, 0, 2))
```

```python
from contextlib import ExitStack

import concourse.bass as bass
from concourse import mybir

F32 = mybir.dt.float32
F32R = mybir.dt.float32r
BF16 = mybir.dt.bfloat16
I32 = mybir.dt.int32
ALU = mybir.AluOpType
ACT = mybir.ActivationFunctionType
AX = mybir.AxisListType

B, N, C = 16, 128, 128
H, HD = 16, 8
F = 4 * C
FC = F // C
G = 4
EPS = 1e-6
MASKED = -1e9
ROWS = 32
MROW = 12

_W = [("cond", B), ("film1", 2 * C), ("film2", 2 * C), ("cols0", 16), ("q", C), ("k", C), ("vt", C),
      ("proj", C), ("x_end", 0), ("mlp1", F), ("mlp2", F), ("m_end", 0), ("ada", 6 * C),
      ("cols1", 16), ("qkv", 3 * C), ("proj1", C), ("fc1", F), ("fc2", F)]
W_AT, _n = {}, 0
for _name, _size in _W:
    W_AT[_name] = _n
    _n += _size
W_ALL = _n
_R = [("proj_b", C), ("mlp_b2", C), ("qk_b", 2 * C), ("proj1_b", C), ("fc2_b", C), ("gate_b", 2 * C)]
R_AT, _n = {}, 0
for _name, _size in _R:
    R_AT[_name] = _n
    _n += _size
R_ALL = _n


def build(nc, x, weights, rows, mask, mask_t, gates, out):
    with ExitStack() as ctx:
        def sb(name, shape, dt=F32):
            return ctx.enter_context(nc.sbuf_tensor(name, shape, dt))

        def sem(name):
            return ctx.enter_context(nc.semaphore(name))

        W = sb("W", [128, W_ALL])
        R = sb("R", [128, R_ALL])
        xs = sb("xs", [N, B, C])
        xb = sb("xb", [N, B, C])
        agg = sb("agg", [N, G, 2])
        mean = sb("mean", [N, 2, B])
        rstd = sb("rstd", [N, 4, B])
        var_eps = sb("var_eps", [N, 4, B])
        mean_sq = sb("mean_sq", [N, G])
        bn = sb("bn", [N, G, 6])
        bn_c = sb("bn_c", [N, 6])
        agg_c = sb("agg_c", [N, 2])
        half = sb("half", [N, B])
        ident = sb("ident", [128, 128])
        identb = sb("identb", [128, 128], BF16)
        xn = [sb(f"xn{u}", [N, G, C]) for u in range(2)]
        hT = [sb(f"hT{u}", [C, G, N]) for u in range(2)]
        scale = sb("scale", [C, 4, B])
        shift = sb("shift", [C, 4, B])
        shared = sb("shared", [128, 8, G, N])
        qT, kT, v0, p0 = ([shared[:, 2 * n + u] for u in range(2)] for n in range(4))
        pT0 = [sb(f"apT{u}", [N, G, N]) for u in range(2)]
        amax = sb("amax", [N, 2, G])
        aden = sb("aden", [N, 2, G])
        arden = sb("arden", [N, 2, G])
        wvp = sb("wvp", [C, C])
        bias_a = sb("bias_a", [N, C])
        bcol = sb("bcol", [C, N])
        hid = [sb(f"hid{u}", [128, FC, G, N]) for u in range(2)]
        gmul = [sb(f"gmul{u}", [N, G, C]) for u in range(2)]
        cond_e = sb("cond_e", [C, B])
        cond_s = sb("cond_s", [C, B])
        cond_r = sb("cond_r", [C, B])
        silu = sb("silu", [C, B])
        gate_rows = sb("gate_rows", [B, 2, C])
        gate = sb("gate", [N, B, 2, C])
        pbias1 = sb("pbias1", [N, C])
        bcol1 = sb("bcol1", [C, N])
        gtmp = sb("gtmp", [N, G, C])
        mask_i = sb("mask_i", [128, B, N], I32)
        maskt_i = sb("maskt_i", [N, B], I32)
        valid = sb("valid", [N, B])
        mod32 = sb("mod32", [128, 32])
        sel_f = sb("sel_f", [128, 4])
        row_amp = sb("row_amp", [128, 1])
        row_neg = sb("row_neg", [128, 1])
        mask_term = sb("mask_term", [128, B, N], BF16)
        sel_base = sb("sel_base", [128, 4, N], BF16)
        upto = sb("upto", [128, 128])
        mask_b = sb("mask_b", [128, B, N], BF16)
        first = sb("first", [N, B])
        nofirst = [sb(f"nofirst{u}", [N, N]) for u in range(2)]
        keep = [sb(f"keep{u}", [N, N]) for u in range(2)]
        turn_k = [sb(f"turn_k{u}", [N, N], F32R) for u in range(2)]
        sel = [sb(f"sel{u}", [128, 4, N], BF16) for u in range(2)]
        xc = [sb(f"xc{u}", [N, C]) for u in range(2)]
        hc = [sb(f"hc{u}", [C, N]) for u in range(2)]
        qbv = [sb(f"qbv{u}", [N, C]) for u in range(2)]
        qk = [sb(f"qk{u}", [N, 2, H, HD]) for u in range(2)]
        qkx = [sb(f"qkx{u}", [N, 2, H, 4, HD]) for u in range(2)]
        qxT = [sb(f"qxT{u}", [128, 4, N], F32R) for u in range(2)]
        kxT = [sb(f"kxT{u}", [128, 4, N], F32R) for u in range(2)]
        qdiag = [sb(f"qdiag{u}", [128, 4, 4, N], F32R) for u in range(2)]
        kdiag = [sb(f"kdiag{u}", [128, 4, 4, N], F32R) for u in range(2)]
        vx = [sb(f"vx{u}", [N, 8 * 64]) for u in range(2)]
        nmax = [sb(f"nmax{u}", [N, 16]) for u in range(2)]
        mrest = [sb(f"mrest{u}", [N, 16]) for u in range(2)]
        nm = [sb(f"nm{u}", [N, 4, 32], BF16) for u in range(2)]
        nmdiag = [sb(f"nmdiag{u}", [128, 4, N], BF16) for u in range(2)]
        pT = [shared[:, 4 * u:4 * u + 4] for u in range(2)]
        oT = [sb(f"oT{u}", [128, 2, N]) for u in range(2)]
        rden = [sb(f"rden{u}", [N, 16]) for u in range(2)]
        on = [sb(f"on{u}", [N, 16, HD]) for u in range(2)]
        onT = [sb(f"onT{u}", [C, N]) for u in range(2)]
        attn = [sb(f"attn{u}", [N, C]) for u in range(2)]
        gated = [sb(f"gated{u}", [N, C]) for u in range(2)]

        ps = ctx.enter_context(nc.psum_tensor("ps", [128, 8, 512], F32))

        def bank(i):
            return ps[:, i, :].rearrange("p (g n) -> p g n", g=G)

        def w(name, size=C, at=0):
            a = W_AT[name] + at
            return W[:, a:a + size]

        def row(name, size=C, at=0):
            a = R_AT[name] + at
            return R[:, a:a + size]

        def col(name, j):
            return w(name, 1, j)

        COL = {"q_b": 0, "k_b": 1, "v_b": 2, "n1": 3, "n2": 4, "film1": 5, "film2": 7, "mlp_b1": 9}
        COL1 = {"ada": 0, "v_b": 6, "fc1": 7}

        names = """settled x_in0 x_in1 x_in2 x_in3 w_film w_attn0 w_ada w_mlp0 w_block1 rows_in mask_in gate_out gate_in y_out
            ident_ok half_ok stats_ok film_mm film_one film_ok silu_e silu_one silu_ok
            ada_mm ada_ok gate_mm gate_ok bias_mm wvp_mm wvp_ok bias_ok bcol_ok pbias_ok
            valid_ok mod32_ok selc_ok mterm_ok selbase_ok upto_ok maskb_ok diag_ok c_first c_keep c_turn c_vinit
            a_pow a_xn a_xb a_T a_h a_Q a_K a_V a_qT a_kT a_v a_S a_max a_exp a_PT a_pT a_PV a_rden a_res
            b_pow b_xn b_xb b_T b_h b_M1 b_gelu b_M2 b_res
            c_pow c_xb c_gp c_nv c_sel c_qbv c_xc c_Tx c_h c_QK c_V c_q c_k c_v c_hiq c_hik c_lo c_Tq c_Tk c_qT c_kT c_qd c_kd
            c_S c_max c_nm c_NT c_nmT c_ST c_exp c_PV c_oT c_T2 c_rden c_on c_T3 c_onT c_pr c_at c_ga c_res c_st
            d_pow d_xn d_xb d_T d_h d_M1 d_gelu d_M2 d_gm d_gp d_res""".split()
        s = {n: sem(n) for n in names}

        PER_GROUP = 2 * G + 2

        def stats_end(k, g):
            return PER_GROUP * (G * k + g + 1)

        def settled(eng):
            eng.sem_inc(s["settled"], 1)

        def batch(t, b):
            return t[:, bass.ds(b, 1), :].rearrange("p a c -> p (a c)")

        block = ctx.enter_context(nc.Block())

        @block.sync
        def _(sp):
            sp.dma_start(xs[:, 0:G], x[:, 0:G]).then_inc(s["x_in0"], 16)
            for n, (a, b) in enumerate((("q", "x_end"), ("ada", "qkv"), ("mlp1", "m_end"), ("qkv", None))):
                a, b = W_AT[a], W_AT[b] if b else W_ALL
                sp.dma_start(W[:, a:b], weights[:, a:b]).then_inc(s[("w_attn0", "w_ada", "w_mlp0", "w_block1")[n]], 16)
                if n == 0:
                    for g in range(1, 4):
                        sp.dma_start(xs[:, G * g:G * g + G], x[:, G * g:G * g + G]).then_inc(s[f"x_in{g}"], 16)
            sp.wait_ge(s["gate_ok"], 1)
            sp.dma_start(gates, gate_rows[:].rearrange("b g c -> b (g c)")).then_inc(s["gate_out"], 16)
            sp.wait_ge(s["gate_out"], 16)
            sp.dma_start(gate[:], gates.rearrange("b f -> (b f)").partition_broadcast(128)).then_inc(s["gate_in"], 16)
            for g in range(4):
                sp.wait_ge(s["d_res"], g + 1)
                sp.dma_start(out[:, G * g:G * g + G], xs[:, G * g:G * g + G]).then_inc(s["y_out"], 16)
            sp.wait_ge(s["y_out"], 64)

        @block.tensor
        def _(pe):
            mm = nc.tensor.matmul

            def transposes(dst, src, signal):
                for j in range(G):
                    ins = nc.tensor.transpose(dst[:, j], src[:, j], ident[:])
                ins.then_inc(signal, 1)

            def a_norm(g):
                pe.wait_ge(s["a_xn"], g + 1)
                transposes(bank(0), xn[g % 2], s["a_T"])

            def a_qkv(g):
                u = g % 2
                pe.wait_ge(s["a_h"], g + 1)
                mm(ps[:, 1, :], w("q"), hT[u][:], start=True, stop=True).then_inc(s["a_Q"], 1)
                mm(ps[:, 2, :], w("k"), hT[u][:], start=True, stop=True).then_inc(s["a_K"], 1)
                pe.wait_ge(s["wvp_ok"], 1)
                for j in range(G):
                    ins = mm(bank(3)[:, j], hT[u][:, j], wvp[:], start=True, stop=True, skip_group_check=True)
                ins.then_inc(s["a_V"], 1)

            def a_scores(g):
                u = g % 2
                pe.wait_ge(s["a_qT"], g + 1)
                pe.wait_ge(s["a_kT"], g + 1)
                for j in range(G):
                    ins = mm(bank(4 + 3 * u)[:, j], qT[u][:, j], kT[u][:, j], start=True, stop=True, skip_group_check=True)
                ins.then_inc(s["a_S"], 1)
                pe.wait_ge(s["a_v"], g + 1)

            def a_turn(g):
                pe.wait_ge(s["a_exp"], G * (g + 1))
                transposes(bank(5), p0[g % 2], s["a_PT"])

            def a_weighted(g):
                pe.wait_ge(s["a_pT"], g + 1)
                if g:
                    pe.wait_ge(s["a_res"], G * g)
                for j in range(G):
                    ins = mm(bank(6)[:, j], pT0[g % 2][:, j], v0[g % 2][:, j], start=True, stop=True, skip_group_check=True)
                ins.then_inc(s["a_PV"], 1)

            def m_norm(p, g, t_bank):
                pe.wait_ge(s[p + "xn"], g + 1)
                if g:
                    pe.wait_ge(s[p + "h"], g)
                transposes(bank(t_bank), xn[g % 2], s[p + "T"])

            def m_up(p, g, w1, h_bank, chunks=range(FC)):
                for f in chunks:
                    if f == 0:
                        pe.wait_ge(s[p + "h"], g + 1)
                    if g:
                        pe.wait_ge(s[p + "gelu"], FC * (g - 1) + f + 1)
                    mm(ps[:, h_bank + f, :], w(w1, C, C * f), hT[g % 2][:], start=True, stop=True).then_inc(s[p + "M1"], 1)

            def m_down(p, g, w2, o_bank):
                pe.wait_ge(s[p + "gelu"], FC * (g + 1))
                if g:
                    pe.wait_ge(s["b_res" if p == "b_" else "d_gm"], g)
                for j in range(G):
                    for f in range(FC):
                        ins = mm(bank(o_bank)[:, j], hid[g % 2][:, f, j], w(w2, C, C * f),
                                 start=(f == 0), stop=(f == FC - 1), skip_group_check=True)
                ins.then_inc(s[p + "M2"], 1)

            def front_a(b, u):
                pe.wait_ge(s["c_xc"], b + 1)
                nc.tensor.transpose(ps[:, 6, 0:N], xc[u][:], ident[:]).then_inc(s["c_Tx"], 1)

            def front_b(b, u):
                pe.wait_ge(s["c_h"], b + 1)
                mm(ps[:, 4, 0:2 * C], hc[u][:], w("qkv", 2 * C), start=True, stop=True).then_inc(s["c_QK"], 1)
                if not isinstance(b, int) or b:
                    pe.wait_ge(s["c_kT"], b)
                mm(ps[:, 7, 0:C], hc[u][:], w("qkv", C, 2 * C), start=True, stop=True).then_inc(s["c_V"], 1)

            def split_rows(u, n, t):
                return qkx[u][:, n].rearrange("n (t r) s d -> n t (r s d)", t=4)[:, t]

            def front_q(b, u):
                pe.wait_ge(s["c_lo"], 2 * b + 1)
                for t in range(4):
                    ins = nc.tensor.transpose(bank(6)[:, t], split_rows(u, 0, t), ident[:])
                ins.then_inc(s["c_Tq"], 1)

            def front_k(b, u):
                pe.wait_ge(s["c_lo"], 2 * b + 2)
                pe.wait_ge(s["c_turn"], b + 1)
                pe.wait_ge(s["c_v"], b + 1)
                for t in range(4):
                    ins = mm(bank(7)[:, t], split_rows(u, 1, t).bitcast(F32R), turn_k[u][:], start=True, stop=True,
                             skip_group_check=True)
                ins.then_inc(s["c_Tk"], 1)

            def scores(b, u, halves, back):
                if 0 in halves:
                    pe.wait_ge(s["c_qT"], b + 1)
                    pe.wait_ge(s["c_kd"], b + 1)
                for t in (t for e in halves for t in (2 * e, 2 * e + 1)):
                    if back and t % 2 == 0:
                        pe.wait_ge(s["c_exp"], 2 * b + t // 2 - 1)
                    ins = mm(ps[:, t, :], qxT[u][:, t], kdiag[u][:, t], start=True, stop=True)
                    if t % 2:
                        ins.then_inc(s["c_S"], 1)

            def scores_t(b, u, e):
                if e == 0:
                    pe.wait_ge(s["c_kT"], b + 1)
                    pe.wait_ge(s["c_qd"], 2 * b + 2)
                pe.wait_ge(s["c_max"], 2 * b + e + 1)
                for t in (2 * e, 2 * e + 1):
                    mm(ps[:, t, :], kxT[u][:, t], qdiag[u][:, t], start=True, stop=False, skip_group_check=True)

            def turn_maxima(b, u):
                pe.wait_ge(s["c_nm"], 4 * b + 4)
                nc.tensor.transpose(ps[:, 4, 256:256 + N // 2].bitcast(BF16), nm[u][:].rearrange("n r k -> n (r k)"),
                                    identb[:]).then_inc(s["c_NT"], 1)

            def subtract_maxima(b, u):
                pe.wait_ge(s["c_nmT"], b + 1)
                pe.wait_ge(s["c_sel"], b + 1)
                for t in range(4):
                    ins = mm(ps[:, t, :], sel[u][:, t], nmdiag[u][:], start=False, stop=True, skip_group_check=True)
                    if t % 2:
                        ins.then_inc(s["c_ST"], 1)

            def weighted(b, u, e):
                pe.wait_ge(s["c_exp"], 2 * b + e + 1)
                if e == 0:
                    pe.wait_ge(s["c_v"], b + 1)
                    if not isinstance(b, int) or b:
                        pe.wait_ge(s["c_on"], b)
                    else:
                        pe.wait_ge(s["b_res"], 4)
                v = vx[u][:].rearrange("n (e j s c) -> n e j s c", e=2, j=4, s=2)
                p = pT[u].rearrange("n (e t) (k s) q -> n e (t k) s q", e=2, k=2)
                for s2 in range(2):
                    for j in range(4):
                        ins = mm(ps[32 * j:32 * j + 32, 5, N * e:N * e + N], v[:, e, j, s2], p[:, e, j, s2],
                                 start=(s2 == 0), stop=(s2 == 1), skip_group_check=True)
                ins.then_inc(s["c_PV"], 1)

            def back_a(b, u):
                pe.wait_ge(s["c_oT"], b + 1)
                for e in range(2):
                    ins = nc.tensor.transpose(ps[:, 5, 128 * e:128 * e + 128], oT[u][:, e], ident[:])
                ins.then_inc(s["c_T2"], 1)

            def back_b(b, u, t_bank=6):
                pe.wait_ge(s["c_on"], b + 1)
                nc.tensor.transpose(ps[:, t_bank, 0:N], on[u][:].rearrange("n h d -> n (h d)"), ident[:]).then_inc(s["c_T3"], 1)

            def back_c(b, u, bank=6):
                pe.wait_ge(s["c_onT"], b + 1)
                mm(ps[:, bank, 2 * N:2 * N + C], onT[u][:], w("proj1"), start=True, stop=True).then_inc(s["c_pr"], 1)

            def step(b, u, end=True, back=True, front=True, ahead=True):
                scores(b, u, (0,), back)
                if end:
                    back_b(b - 2, u)
                scores(b, u, (1,), back)
                if end:
                    back_c(b - 2, u)
                if back:
                    weighted(b - 1, 1 - u, 0)
                    weighted(b - 1, 1 - u, 1)
                scores_t(b, u, 0)
                if front:
                    if end:
                        pe.wait_ge(s["c_at"], b - 1)
                    front_q(b + 1, 1 - u)
                scores_t(b, u, 1)
                if back:
                    back_a(b - 1, 1 - u)
                if front:
                    pe.wait_ge(s["c_k"], b + 2)
                turn_maxima(b, u)
                if front:
                    front_k(b + 1, 1 - u)
                if ahead:
                    pe.wait_ge(s["c_qT"], b + 2)
                    front_a(b + 2, u)
                subtract_maxima(b, u)
                if ahead:
                    front_b(b + 2, u)

            pe.wait_ge(s["w_film"], 16)
            for j in range(4):
                ins = mm(ps[:, 7, B * j:B * j + B], w(("film1", "film2")[j // 2], C, C * (j % 2)), w("cond", B),
                         start=(j == 0), stop=True, skip_group_check=True)
            ins.then_inc(s["film_mm"], 1)
            pe.wait_ge(s["ident_ok"], 4)
            a_norm(0)
            pe.wait_ge(s["w_attn0"], 16)
            mm(ps[:, 6, 0:C], w("vt"), w("proj"), start=True, stop=True).then_inc(s["wvp_mm"], 1)
            pe.wait_ge(s["bcol_ok"], 1)
            mm(ps[:, 5, 0:C], bcol[:], w("proj"), start=True, stop=True).then_inc(s["wvp_mm"], 1)
            a_qkv(0)
            a_norm(1)
            a_scores(0)
            for g in range(4):
                if g < 3:
                    a_qkv(g + 1)
                else:
                    m_norm("b_", 0, 0)
                if g == 0:
                    pe.wait_ge(s["bias_ok"], 1)
                a_turn(g)
                if g < 2:
                    a_norm(g + 2)
                if g < 3:
                    a_scores(g + 1)
                a_weighted(g)

            m_norm("b_", 1, 0)
            pe.wait_ge(s["w_mlp0"], 16)
            m_up("b_", 0, "mlp1", 1)
            pe.wait_ge(s["a_res"], B)
            pe.wait_ge(s["w_ada"], 16)
            pe.wait_ge(s["silu_ok"], 1)
            for n, j in enumerate((1, 4, 0, 3)):
                ins = mm(ps[:, 6, B * n:B * n + B], w("ada", C, C * j), silu[:], start=(n == 0), stop=True,
                         skip_group_check=True)
            pe.wait_ge(s["upto_ok"], 2)
            pe.wait_ge(s["valid_ok"], 1)
            ins = mm(ps[:, 6, 4 * B:5 * B], upto[:], valid[:], start=False, stop=True, skip_group_check=True)
            ins.then_inc(s["ada_mm"], 1)
            for n, j in enumerate((2, 5)):
                ins = mm(ps[0:B, 7, C * n:C * n + C], silu[:], w("ada", C, C * j), start=(n == 0), stop=True,
                         skip_group_check=True)
            ins.then_inc(s["gate_mm"], 1)
            m_up("b_", 1, "mlp1", 1)
            pe.wait_ge(s["ada_ok"], 1)
            pe.wait_ge(s["w_block1"], 16)
            pe.wait_ge(s["bcol_ok"], 2)
            mm(ps[:, 6, 0:C], bcol1[:], w("proj1"), start=True, stop=True).then_inc(s["bias_mm"], 1)
            m_norm("b_", 2, 0)
            m_down("b_", 0, "mlp2", 5)
            m_up("b_", 2, "mlp1", 1)
            m_norm("b_", 3, 0)
            m_down("b_", 1, "mlp2", 5)
            m_up("b_", 3, "mlp1", 1)
            m_down("b_", 2, "mlp2", 5)
            pe.wait_ge(s["pbias_ok"], 1)
            pe.wait_ge(s["gate_ok"], 1)
            front_a(0, 0)
            pe.wait_ge(s["b_gelu"], 4 * FC)
            front_b(0, 0)
            m_down("b_", 3, "mlp2", 5)
            front_q(0, 0)
            front_k(0, 0)
            pe.wait_ge(s["c_qT"], 1)
            front_a(1, 1)
            pe.wait_ge(s["c_k"], 1)
            front_b(1, 1)

            pe.wait_ge(s["c_vinit"], 10)
            step(0, 0, end=False, back=False)
            step(1, 1, end=False)
            with pe.Fori(0, B // 2 - 2) as i:
                step(2 * i + 2, 0)
                step(2 * i + 3, 1)
            step(B - 2, 0, ahead=False)
            step(B - 1, 1, front=False, ahead=False)

            back_b(B - 2, 0, 4)
            back_c(B - 2, 0, 4)
            m_norm("d_", 0, 6)
            weighted(B - 1, 1, 0)
            weighted(B - 1, 1, 1)
            m_norm("d_", 1, 6)
            back_a(B - 1, 1)
            m_up("d_", 0, "fc1", 0, range(2))
            back_b(B - 1, 1, 4)
            m_up("d_", 0, "fc1", 0, range(2, 4))
            back_c(B - 1, 1, 4)
            m_up("d_", 1, "fc1", 0)
            m_norm("d_", 2, 6)
            m_down("d_", 0, "fc2", 7)
            m_up("d_", 2, "fc1", 0)
            m_norm("d_", 3, 6)
            m_down("d_", 1, "fc2", 7)
            m_up("d_", 3, "fc1", 0)
            m_down("d_", 2, "fc2", 7)
            m_down("d_", 3, "fc2", 7)

        @block.scalar
        def _(act):
            a = nc.scalar.activation
            act.dma_start(W[:, 0:W_AT["q"]], weights[:, 0:W_AT["q"]]).then_inc(s["w_film"], 16)
            act.dma_start(R[:, :], rows.partition_broadcast(128)).then_inc(s["rows_in"], 16)
            act.dma_start(mask_i[:], mask.rearrange("b n -> (b n)").partition_broadcast(128)).then_inc(s["mask_in"], 16)
            act.dma_start(maskt_i[:], mask_t).then_inc(s["mask_in"], 16)
            act.wait_ge(s["w_film"], 16)
            a(cond_e[:], w("cond", B), ACT.Exp, scale=-1.0).then_inc(s["silu_e"], 1)

            def affine(p, g, k, src):
                act.wait_ge(s[p + "T"], g + 1)
                for j in range(G):
                    b = G * g + j
                    ins = a(hT[g % 2][:, j], src[:, j], ACT.Identity, bias=shift[:, k, b:b + 1],
                            scale=scale[:, k, b:b + 1])
                ins.then_inc(s[p + "h"], 1)

            def a_kv(g):
                act.wait_ge(s["a_K"], g + 1)
                a(kT[g % 2][:], bank(2), ACT.Identity, bias=col("cols0", COL["k_b"])).then_inc(s["a_kT"], 1)
                act.wait_ge(s["a_V"], g + 1)
                a(v0[g % 2][:], bank(3), ACT.Copy).then_inc(s["a_v"], 1)

            def a_exp(g):
                u = g % 2
                act.wait_ge(s["a_max"], g + 1)
                for j in range(G):
                    a(p0[u][:, j], bank(4 + 3 * u)[:, j], ACT.Exp, bias=amax[:, u, j:j + 1],
                      accum_out=aden[:, u, j:j + 1]).then_inc(s["a_exp"], 1)

            act.wait_ge(s["film_ok"], 2)
            affine("a_", 0, 0, bank(0))
            act.wait_ge(s["wvp_mm"], 1)
            a(wvp[:], ps[:, 6, 0:C], ACT.Copy).then_inc(s["wvp_ok"], 1)
            a_kv(0)
            affine("a_", 1, 0, bank(0))
            a_exp(0)
            for g in range(1, 4):
                a_kv(g)
                if g < 3:
                    affine("a_", g + 1, 0, bank(0))
                a_exp(g)

            def gelus(p, g, func, bcols, bat, h_bank):
                for f in range(FC):
                    act.wait_ge(s[p + "M1"], FC * g + f + 1)
                    if g > 1:
                        act.wait_ge(s[p + "M2"], g - 1)
                    a(hid[g % 2][:, f], bank(h_bank + f), func, bias=col(bcols, bat + f)).then_inc(s[p + "gelu"], 1)

            affine("b_", 0, 1, bank(0))
            affine("b_", 1, 1, bank(0))
            gelus("b_", 0, ACT.Gelu, "cols0", COL["mlp_b1"], 1)
            gelus("b_", 1, ACT.Gelu, "cols0", COL["mlp_b1"], 1)
            affine("b_", 2, 1, bank(0))
            gelus("b_", 2, ACT.Gelu, "cols0", COL["mlp_b1"], 1)
            affine("b_", 3, 1, bank(0))
            gelus("b_", 3, ACT.Gelu, "cols0", COL["mlp_b1"], 1)

            def front_h(b, u):
                act.wait_ge(s["c_Tx"], b + 1)
                act.wait_ge(s["ada_ok"], 1)
                a(hc[u][:], ps[:, 6, 0:N], ACT.Identity, bias=shift[:, 2, bass.ds(b, 1)],
                  scale=scale[:, 2, bass.ds(b, 1)]).then_inc(s["c_h"], 1)

            def front_v(b, u):
                act.wait_ge(s["c_V"], b + 1)
                v = ps[:, 7, 0:C].rearrange("n (a k d) -> n a k d", k=2, d=HD)
                slots = vx[u][:].rearrange("n (a z) -> n a z", z=64)
                for k in range(2):
                    ins = a(slots[:, :, 48 * k:48 * k + HD], v[:, :, k], ACT.Copy)
                ins.then_inc(s["c_v"], 1)

            def front_hi(b, u):
                for n, (ready, slots, signal) in enumerate((("c_q", slice(0, 2), "c_hiq"), ("c_k", slice(0, 4, 2), "c_hik"))):
                    act.wait_ge(s[ready], b + 1)
                    a(qkx[u][:, n, :, slots].bitcast(F32R), qk[u][:, n].unsqueeze(2).broadcast_to((N, H, 2, HD)),
                      ACT.Copy).then_inc(s[signal], 1)

            def front_q(b, u):
                act.wait_ge(s["c_Tq"], b + 1)
                a(qxT[u][:], bank(6), ACT.Copy).then_inc(s["c_qT"], 1)

            def front_k(b, u):
                act.wait_ge(s["c_Tk"], b + 1)
                a(kxT[u][:], bank(7), ACT.Copy).then_inc(s["c_kT"], 1)

            def front_qdiag(b, u, rs):
                act.wait_ge(s["c_qT"], b + 1)
                for r in rs:
                    rows = slice(32 * r, 32 * r + 32)
                    ins = a(qdiag[u][rows, :, r], qxT[u][rows], ACT.Copy)
                ins.then_inc(s["c_qd"], 1)

            def weights_of(b, u, e):
                act.wait_ge(s["c_ST"], 2 * b + e + 1)
                a(pT[u][:, 2 * e:2 * e + 2], ps[:, 2 * e:2 * e + 2, :].rearrange("n t (r q) -> n t r q", r=4),
                  ACT.Exp, scale=HD ** -0.5).then_inc(s["c_exp"], 1)

            def turned_o(b, u, t_bank=6):
                act.wait_ge(s["c_T3"], b + 1)
                a(onT[u][:], ps[:, t_bank, 0:N], ACT.Copy).then_inc(s["c_onT"], 1)

            def back_o(b, u):
                act.wait_ge(s["c_PV"], 2 * b + 2)
                a(oT[u][:], ps[:, 5, 0:2 * N].rearrange("p (e n) -> p e n", e=2), ACT.Copy).then_inc(s["c_oT"], 1)

            def projected(b, u, bank=6):
                act.wait_ge(s["c_pr"], b + 1)
                a(attn[u][:], ps[:, bank, 2 * N:2 * N + C], ACT.Copy).then_inc(s["c_at"], 1)

            def step(b, u, end=True, back=True, front=True, ahead=True):
                if end:
                    turned_o(b - 2, u)
                front_qdiag(b, u, (2, 3))
                if end:
                    projected(b - 2, u)
                if front:
                    front_hi(b + 1, 1 - u)
                if back:
                    back_o(b - 1, 1 - u)
                if front:
                    front_v(b + 1, 1 - u)
                    front_q(b + 1, 1 - u)
                    front_qdiag(b + 1, 1 - u, (0, 1))
                    front_k(b + 1, 1 - u)
                if ahead:
                    front_h(b + 2, u)
                weights_of(b, u, 0)
                weights_of(b, u, 1)

            front_h(0, 0)
            act.wait_ge(s["c_vinit"], 6)
            front_v(0, 0)
            front_hi(0, 0)
            front_q(0, 0)
            front_k(0, 0)
            act.wait_ge(s["diag_ok"], 4)
            front_qdiag(0, 0, (0, 1))
            front_h(1, 1)
            step(0, 0, end=False, back=False)
            step(1, 1, end=False)
            with act.Fori(0, B // 2 - 2) as i:
                step(2 * i + 2, 0)
                step(2 * i + 3, 1)
            step(B - 2, 0, ahead=False)
            step(B - 1, 1, front=False, ahead=False)
            turned_o(B - 2, 0, 4)
            projected(B - 2, 0, 4)
            affine("d_", 0, 3, bank(6))
            back_o(B - 1, 1)
            affine("d_", 1, 3, bank(6))
            gelus("d_", 0, ACT.Gelu_apprx_tanh, "cols1", COL1["fc1"], 0)
            gelus("d_", 1, ACT.Gelu_apprx_tanh, "cols1", COL1["fc1"], 0)
            affine("d_", 2, 3, bank(6))
            gelus("d_", 2, ACT.Gelu_apprx_tanh, "cols1", COL1["fc1"], 0)
            affine("d_", 3, 3, bank(6))
            gelus("d_", 3, ACT.Gelu_apprx_tanh, "cols1", COL1["fc1"], 0)

        @block.vector
        def _(dve):
            v = nc.vector
            v.memset(half[:], -0.5).then_inc(s["half_ok"], 1)

            def statistics(k, g):
                ok = s["stats_ok"]
                base = stats_end(k, g) - PER_GROUP
                if base:
                    dve.wait_ge(ok, base)
                for j in range(G):
                    v.bn_stats(bn[:, j], xs[:, G * g + j]).then_inc(ok, 1)
                for j in range(G):
                    dve.wait_ge(ok, base + j + 1)
                    v.bn_aggr(agg[:, j], bn[:, j]).then_inc(ok, 1)
                ve = var_eps[:, k, G * g:G * g + G]
                dve.wait_ge(ok, base + 2 * G)
                if k < 2:
                    v.tensor_tensor(mean_sq[:], agg[:, :, 0], agg[:, :, 0], ALU.mult).then_inc(ok, 1)
                    dve.wait_ge(ok, base + 2 * G + 1)
                    v.scalar_tensor_tensor(out=ve, in0=agg[:, :, 1], scalar=EPS, in1=mean_sq[:], op0=ALU.add, op1=ALU.add)\
                        .then_inc(ok, 1)
                else:
                    v.tensor_copy(mean[:, 0, G * g:G * g + G], agg[:, :, 0]).then_inc(ok, 1)
                    v.tensor_scalar(ve, agg[:, :, 1], EPS, None, ALU.add).then_inc(ok, 1)

            def m_norm(p, k, g):
                dve.wait_ge(s[p + "pow"], g + 1)
                if g > 1:
                    dve.wait_ge(s[p + "T"], g - 1)
                for j in range(G):
                    b = G * g + j
                    if k == 1:
                        ins = v.tensor_scalar(xn[g % 2][:, j], xs[:, b], rstd[:, 1, b:b + 1], None, ALU.mult)
                    else:
                        ins = v.tensor_scalar(xn[g % 2][:, j], xs[:, b], mean[:, 1, b:b + 1], rstd[:, 3, b:b + 1],
                                              ALU.subtract, ALU.mult)
                ins.then_inc(s[p + "xn"], 1)

            dve.wait_ge(s["x_in0"], 16)
            statistics(0, 0)
            dve.wait_ge(s["film_mm"], 1)
            for k, c in enumerate(("film1", "film2")):
                v.tensor_scalar(scale[:, k, :], ps[:, 7, 2 * B * k:2 * B * k + B], col("cols0", COL[c]), 1.0,
                                ALU.add, ALU.add).then_inc(s["film_one"], 1)
                v.tensor_scalar(shift[:, k, :], ps[:, 7, 2 * B * k + B:2 * B * k + 2 * B],
                                col("cols0", COL[c] + 1), None, ALU.add).then_inc(s["film_one"], 1)
            dve.wait_ge(s["film_one"], 4)
            for k, n in enumerate(("n1", "n2")):
                v.tensor_scalar(scale[:, k, :], scale[:, k, :], col("cols0", COL[n]), None, ALU.mult)\
                    .then_inc(s["film_ok"], 1)
            dve.wait_ge(s["x_in1"], 16)
            statistics(0, 1)
            dve.wait_ge(s["wvp_mm"], 2)
            dve.wait_ge(s["rows_in"], 16)
            v.tensor_tensor(bias_a[:], ps[:, 5, 0:C], row("proj_b"), ALU.add).then_inc(s["bias_ok"], 1)

            def a_q(g):
                dve.wait_ge(s["a_Q"], g + 1)
                v.tensor_scalar(qT[g % 2][:], bank(1), col("cols0", COL["q_b"]), C ** -0.5, ALU.add, ALU.mult)\
                    .then_inc(s["a_qT"], 1)

            def a_max(g):
                u = g % 2
                dve.wait_ge(s["a_S"], g + 1)
                v.tensor_reduce(amax[:, u, :], bank(4 + 3 * u), AX.X, ALU.max, negate=True).then_inc(s["a_max"], 1)

            def a_turn(g):
                dve.wait_ge(s["a_PT"], g + 1)
                v.tensor_copy(pT0[g % 2][:], bank(5)).then_inc(s["a_pT"], 1)

            def a_residual(g):
                u = g % 2
                dve.wait_ge(s["a_exp"], G * (g + 1))
                v.reciprocal(arden[:, u, :], aden[:, u, :]).then_inc(s["a_rden"], 1)
                dve.wait_ge(s["a_rden"], g + 1)
                dve.wait_ge(s["a_xb"], g + 1)
                dve.wait_ge(s["a_PV"], g + 1)
                for j in range(G):
                    b = G * g + j
                    v.scalar_tensor_tensor(out=xs[:, b], in0=bank(6)[:, j], scalar=arden[:, u, j:j + 1], in1=xb[:, b],
                                           op0=ALU.mult, op1=ALU.add).then_inc(s["a_res"], 1)

            a_q(0)
            a_max(0)
            for g in range(4):
                if g < 3:
                    a_q(g + 1)
                if g < 2:
                    dve.wait_ge(s[f"x_in{g + 2}"], 16)
                    statistics(0, g + 2)
                a_turn(g)
                if g < 3:
                    a_max(g + 1)
                if g == 3:
                    dve.wait_ge(s["a_res"], 8)
                    statistics(1, 1)
                a_residual(g)
                if g == 0:
                    dve.wait_ge(s["silu_e"], 1)
                    v.tensor_scalar(cond_s[:], cond_e[:], 1.0, None, ALU.add).then_inc(s["silu_one"], 1)
                    dve.wait_ge(s["silu_one"], 1)
                    v.reciprocal(cond_r[:], cond_s[:]).then_inc(s["silu_one"], 1)
                    dve.wait_ge(s["silu_one"], 2)
                    v.tensor_tensor(silu[:], w("cond", B), cond_r[:], ALU.mult).then_inc(s["silu_ok"], 1)
                if g == 1:
                    dve.wait_ge(s["a_res"], 4)
                    statistics(1, 0)
                if g == 2:
                    m_norm("b_", 1, 0)
            m_norm("b_", 1, 1)

            def b_residual(g):
                b = G * g
                dve.wait_ge(s["b_M2"], g + 1)
                dve.wait_ge(s["b_xb"], g + 1)
                v.tensor_tensor(xs[:, b:b + G], bank(5), xb[:, b:b + G], ALU.add).then_inc(s["b_res"], 1)
                dve.wait_ge(s["b_res"], g + 1)
                statistics(2, g)

            def d_residual(g):
                b = G * g
                dve.wait_ge(s["d_M2"], g + 1)
                if g > 1:
                    dve.wait_ge(s["d_res"], g - 1)
                v.tensor_tensor(gmul[g % 2][:], bank(7), gate[:, b:b + G, 1, :], ALU.mult).then_inc(s["d_gm"], 1)
                dve.wait_ge(s["d_gm"], g + 1)
                dve.wait_ge(s["d_xb"], g + 1)
                v.tensor_tensor(xs[:, b:b + G], gmul[g % 2][:], xb[:, b:b + G], ALU.add).then_inc(s["d_res"], 1)

            dve.wait_ge(s["a_res"], 12)
            statistics(1, 2)
            m_norm("b_", 1, 2)
            dve.wait_ge(s["a_res"], 16)
            statistics(1, 3)
            dve.wait_ge(s["mask_in"], 32)
            v.tensor_copy(valid[:], maskt_i[:]).then_inc(s["valid_ok"], 1)
            dve.wait_ge(s["valid_ok"], 1)
            dve.wait_ge(s["ada_mm"], 1)
            v.scalar_tensor_tensor(out=first[:], in0=ps[:, 6, 4 * B:5 * B], scalar=1.0, in1=valid[:], op0=ALU.is_equal,
                                   op1=ALU.mult)
            for n, j in enumerate((1, 4, 0, 3)):
                dst = scale[:, 2 + n, :] if n < 2 else shift[:, n, :]
                ins = v.tensor_scalar(dst, ps[:, 6, B * n:B * n + B], col("cols1", COL1["ada"] + j),
                                      1.0 if n < 2 else 0.0, ALU.add, ALU.add)
            ins.then_inc(s["ada_ok"], 1)
            dve.wait_ge(s["gate_mm"], 1)
            v.tensor_tensor(gate_rows[:].rearrange("b g c -> b (g c)"), ps[0:B, 7, 0:2 * C], row("gate_b", 2 * C)[0:B, :],
                            ALU.add).then_inc(s["gate_ok"], 1)
            dve.wait_ge(s["ident_ok"], 4)
            v.tensor_reduce(mod32[:], ident[:].rearrange("p (r k) -> p k r", r=4), AX.X, ALU.add).then_inc(s["mod32_ok"], 1)
            dve.wait_ge(s["mod32_ok"], 1)
            v.tensor_reduce(sel_f[:], mod32[:, 0:12].rearrange("p (k t) -> p t k", t=4), AX.X, ALU.add)
            v.tensor_scalar(row_amp[:], mod32[:, MROW:MROW + 1], -MASKED, None, ALU.mult)
            v.tensor_scalar(row_neg[:], mod32[:, MROW:MROW + 1], MASKED, None, ALU.mult).then_inc(s["selc_ok"], 1)
            dve.wait_ge(s["bias_mm"], 1)
            v.tensor_tensor(pbias1[:], ps[:, 6, 0:C], row("proj1_b"), ALU.add).then_inc(s["pbias_ok"], 1)
            b_residual(0)
            m_norm("b_", 1, 3)
            b_residual(1)
            b_residual(2)

            def front_x(b, u):
                if not isinstance(b, int) or b >= 2:
                    dve.wait_ge(s["c_Tx"], b - 1)
                settled(dve)
                v.tensor_scalar(xc[u][:], batch(xs, b), mean[:, 0, bass.ds(b, 1)], rstd[:, 2, bass.ds(b, 1)],
                                ALU.subtract, ALU.mult).then_inc(s["c_xc"], 1)

            def front_qk(b, u):
                dve.wait_ge(s["c_QK"], b + 1)
                dve.wait_ge(s["c_qbv"], b + 1)
                settled(dve)
                v.scalar_tensor_tensor(out=qk[u][:, 0].rearrange("n h d -> n (h d)"), in0=ps[:, 4, 0:C],
                                       scalar=valid[:, bass.ds(b, 1)], in1=qbv[u][:], op0=ALU.mult, op1=ALU.add)\
                    .then_inc(s["c_q"], 1)
                v.tensor_tensor(qk[u][:, 1].rearrange("n h d -> n (h d)"), ps[:, 4, C:2 * C], row("qk_b", C, C), ALU.add)\
                    .then_inc(s["c_k"], 1)

            def front_kdiag(b, u):
                dve.wait_ge(s["c_kT"], b + 1)
                for r in range(4):
                    rows = slice(32 * r, 32 * r + 32)
                    ins = v.tensor_copy(kdiag[u][rows, :, r], kxT[u][rows])
                ins.then_inc(s["c_kd"], 1)

            def maxima(b, u, e):
                dve.wait_ge(s["c_S"], 2 * b + e + 1)
                v.tensor_reduce(nmax[u][:, 8 * e:8 * e + 8],
                                ps[:, 2 * e:2 * e + 2, :].rearrange("n t (r k) -> n (t r) k", r=4), AX.X, ALU.max,
                                negate=True).then_inc(s["c_max"], 1)

            def split_max(b, u):
                m = nmax[u][:].rearrange("n (t r) -> n r t", r=4)
                rest = mrest[u][:].rearrange("n (t r) -> n r t", r=4)
                dve.wait_ge(s["c_max"], 2 * b + 2)
                settled(dve)
                v.tensor_scalar(nm[u][:, :, 0:4], m, valid[:, bass.ds(b, 1)], None, ALU.mult).then_inc(s["c_nm"], 1)
                dve.wait_ge(s["c_nm"], 4 * b + 1)
                settled(dve)
                v.scalar_tensor_tensor(out=rest, in0=m, scalar=valid[:, bass.ds(b, 1)], in1=nm[u][:, :, 0:4],
                                       op0=ALU.mult, op1=ALU.subtract).then_inc(s["c_nm"], 1)
                dve.wait_ge(s["c_nm"], 4 * b + 2)
                v.tensor_copy(nm[u][:, :, 4:8], rest).then_inc(s["c_nm"], 1)
                dve.wait_ge(s["c_nm"], 4 * b + 3)
                v.tensor_tensor(nm[u][:, :, 8:12], rest, nm[u][:, :, 4:8], ALU.subtract).then_inc(s["c_nm"], 1)

            def turned_max(b, u):
                dve.wait_ge(s["c_NT"], b + 1)
                for r in range(4):
                    rows = slice(32 * r, 32 * r + 32)
                    ins = v.tensor_copy(nmdiag[u][rows, r], ps[rows, 4, 256:256 + N // 2].bitcast(BF16))
                ins.then_inc(s["c_nmT"], 1)

            def reciprocals(b, u):
                dve.wait_ge(s["c_T2"], b + 1)
                v.reciprocal(rden[u][:], ps[:, 5, 0:256].rearrange("n (h z) -> n h z", z=16)[:, :, HD]).then_inc(s["c_rden"], 1)

            def normalise(b, u):
                o = ps[:, 5, 0:256].rearrange("n (h z) -> n h z", z=16)
                dve.wait_ge(s["c_rden"], b + 1)
                v.tensor_tensor(on[u][:], o[:, :, 0:HD], rden[u][:].unsqueeze(2).broadcast_to((N, 16, HD)), ALU.mult)\
                    .then_inc(s["c_on"], 1)

            def turned_o(b, u):
                dve.wait_ge(s["c_T3"], b + 1)
                v.tensor_copy(onT[u][:], ps[:, 4, 0:N]).then_inc(s["c_onT"], 1)

            def statistics_1(b):
                dve.wait_ge(s["c_res"], b + 1)
                settled(dve)
                v.bn_stats(bn_c[:], batch(xs, b)).then_inc(s["c_st"], 1)

            def statistics_2(b):
                dve.wait_ge(s["c_st"], 4 * b + 1)
                settled(dve)
                v.bn_aggr(agg_c[:], bn_c[:]).then_inc(s["c_st"], 1)

            def statistics_3(b):
                dve.wait_ge(s["c_st"], 4 * b + 2)
                settled(dve)
                v.tensor_copy(mean[:, 1, bass.ds(b, 1)], agg_c[:, 0:1]).then_inc(s["c_st"], 1)
                v.tensor_scalar(var_eps[:, 3, bass.ds(b, 1)], agg_c[:, 1:2], EPS, None, ALU.add).then_inc(s["c_st"], 1)

            def next_statistics(b):
                statistics_1(b)
                statistics_2(b)
                statistics_3(b)

            def step(b, u, end=True, back=True, front=True, ahead=True):
                maxima(b, u, 0)
                maxima(b, u, 1)
                split_max(b, u)
                if ahead:
                    front_x(b + 2, u)
                turned_max(b, u)
                if end:
                    statistics_1(b - 2)
                if front:
                    front_kdiag(b + 1, 1 - u)
                if back:
                    reciprocals(b - 1, 1 - u)
                if end:
                    statistics_2(b - 2)
                if back:
                    normalise(b - 1, 1 - u)
                if end:
                    statistics_3(b - 2)
                if ahead:
                    front_qk(b + 2, u)

            dve.wait_ge(s["c_pow"], 1)
            front_x(0, 0)
            front_qk(0, 0)
            b_residual(3)
            dve.wait_ge(s["diag_ok"], 4)
            front_x(1, 1)
            front_kdiag(0, 0)
            front_qk(1, 1)
            dve.wait_ge(s["c_pow"], 4)
            step(0, 0, end=False, back=False)
            step(1, 1, end=False)
            with dve.Fori(0, B // 2 - 2) as i:
                step(2 * i + 2, 0)
                step(2 * i + 3, 1)
            step(B - 2, 0, ahead=False)
            step(B - 1, 1, front=False, ahead=False)
            m_norm("d_", 3, 0)
            m_norm("d_", 3, 1)
            next_statistics(B - 2)
            reciprocals(B - 1, 1)
            normalise(B - 1, 1)
            turned_o(B - 1, 1)
            dve.wait_ge(s["c_pr"], B)
            v.tensor_copy(attn[1][:], ps[:, 4, 2 * N:2 * N + C]).then_inc(s["c_at"], 1)
            m_norm("d_", 3, 2)
            next_statistics(B - 1)
            d_residual(0)
            m_norm("d_", 3, 3)
            d_residual(1)
            d_residual(2)
            d_residual(3)

        @block.gpsimd
        def _(pool):
            p = nc.gpsimd
            for m in (ident, identb):
                p.memset(m[:], 0.0).then_inc(s["ident_ok"], 1)
            pool.wait_ge(s["ident_ok"], 2)
            for m in (ident, identb):
                p.affine_select(out=m[:], in_=m[:], compare_op=ALU.not_equal, fill=1.0, base=0,
                                pattern=[[-1, 128]], channel_multiplier=1).then_inc(s["ident_ok"], 1)

            p.memset(upto[:], 1.0).then_inc(s["upto_ok"], 1)
            pool.wait_ge(s["upto_ok"], 1)
            p.affine_select(out=upto[:], in_=upto[:], compare_op=ALU.is_ge, fill=0.0, base=0,
                            pattern=[[1, 128]], channel_multiplier=-1).then_inc(s["upto_ok"], 1)

            def root(k, g, signal):
                if k < 3:
                    pool.wait_ge(s["stats_ok"], stats_end(k, g))
                else:
                    pool.wait_ge(s["c_st"], 4 * G * (g + 1))
                pool.wait_ge(s["half_ok"], 1)
                p.tensor_tensor(rstd[:, k, G * g:G * g + G], var_eps[:, k, G * g:G * g + G], half[:, 0:G], ALU.pow)\
                    .then_inc(signal, 1)

            def bias_add(g, bias, signal):
                b = G * g
                p.tensor_tensor(xb[:, b:b + G], xs[:, b:b + G], bias.unsqueeze(1).broadcast_to((N, G, C)), ALU.add)\
                    .then_inc(signal, 1)

            def a_norm(g):
                root(0, g, s["a_pow"])
                pool.wait_ge(s["a_pow"], g + 1)
                if g > 1:
                    pool.wait_ge(s["a_T"], g - 1)
                for j in range(G):
                    b = G * g + j
                    ins = p.tensor_scalar(xn[g % 2][:, j], xs[:, b], rstd[:, 0, b:b + 1], 0.0, ALU.mult, ALU.add)
                ins.then_inc(s["a_xn"], 1)

            a_norm(0)
            pool.wait_ge(s["ident_ok"], 4)
            pool.wait_ge(s["w_film"], 16)
            p.tensor_scalar(bcol[:], ident[:], 0.0, col("cols0", COL["v_b"]), ALU.mult, ALU.add).then_inc(s["bcol_ok"], 1)
            a_norm(1)
            pool.wait_ge(s["bias_ok"], 1)
            bias_add(0, bias_a[:], s["a_xb"])
            a_norm(2)
            bias_add(1, bias_a[:], s["a_xb"])
            a_norm(3)
            bias_add(2, bias_a[:], s["a_xb"])
            bias_add(3, bias_a[:], s["a_xb"])

            root(1, 0, s["b_pow"])
            pool.wait_ge(s["w_ada"], 16)
            p.tensor_scalar(bcol1[:], ident[:], 0.0, col("cols1", COL1["v_b"]), ALU.mult, ALU.add).then_inc(s["bcol_ok"], 1)
            root(1, 1, s["b_pow"])
            root(1, 2, s["b_pow"])
            root(1, 3, s["b_pow"])
            for g in range(4):
                pool.wait_ge(s["a_res"], G * (g + 1))
                bias_add(g, row("mlp_b2"), s["b_xb"])

            for u in range(2):
                p.memset(vx[u][:], 0.0).then_inc(s["c_vinit"], 1)
                p.memset(nm[u][:], 0.0).then_inc(s["c_vinit"], 1)
                p.memset(nmdiag[u][:], 0.0).then_inc(s["c_vinit"], 1)
            pool.wait_ge(s["c_vinit"], 6)
            for u in range(2):
                for k in range(2):
                    z = vx[u][:].rearrange("n (a z) -> n a z", z=64)[:, :, 48 * k + HD:48 * k + HD + 1]
                    p.memset(z, 1.0).then_inc(s["c_vinit"], 1)
            for m in qdiag + kdiag:
                p.memset(m[:].bitcast(F32), 0.0).then_inc(s["diag_ok"], 1)
            pool.wait_ge(s["mask_in"], 32)
            p.tensor_scalar(mask_b[:].rearrange("p b n -> p (b n)"), mask_i[:].rearrange("p b n -> p (b n)"), 1.0, 0.0,
                            ALU.mult, ALU.add).then_inc(s["maskb_ok"], 1)
            pool.wait_ge(s["selc_ok"], 1)
            p.tensor_scalar(mask_term[:].rearrange("p b n -> p (b n)"), mask_i[:].rearrange("p b n -> p (b n)"),
                            row_amp[:, 0:1], row_neg[:, 0:1], ALU.mult, ALU.add).then_inc(s["mterm_ok"], 1)
            root(2, 0, s["c_pow"])
            p.tensor_copy(sel_base[:], sel_f[:].unsqueeze(2).broadcast_to((128, 4, N))).then_inc(s["selbase_ok"], 1)

            def prepare(b, u):
                settled(pool)
                p.tensor_tensor(qbv[u][:], row("qk_b"), valid[:, bass.ds(b, 1)].broadcast_to((N, C)), ALU.mult)\
                    .then_inc(s["c_qbv"], 1)
                one = first[:, bass.ds(b, 1)].broadcast_to((N, N))
                p.tensor_tensor(nofirst[u][:], ident[:], one, ALU.subtract).then_inc(s["c_first"], 1)
                p.tensor_tensor(gtmp[:, u], gate[:, bass.ds(b, 1), 0, :].rearrange("p a c -> p (a c)"), pbias1[:], ALU.mult)\
                    .then_inc(s["c_gp"], 1)
                pool.wait_ge(s["c_first"], b + 1)
                settled(pool)
                p.tensor_tensor(keep[u][:], nofirst[u][:], mask_b[:, bass.ds(b, 1), :].rearrange("p a n -> p (a n)"),
                                ALU.mult).then_inc(s["c_keep"], 1)
                pool.wait_ge(s["c_gp"], b + 1)
                settled(pool)
                p.tensor_tensor(batch(xb, b), batch(xs, b), gtmp[:, u], ALU.add).then_inc(s["c_xb"], 1)
                pool.wait_ge(s["c_keep"], b + 1)
                settled(pool)
                p.tensor_tensor(turn_k[u][:], keep[u][:], one, ALU.add).then_inc(s["c_turn"], 1)
                if not isinstance(b, int) or b >= 2:
                    pool.wait_ge(s["c_ST"], 2 * b - 2)
                    settled(pool)
                p.tensor_tensor(sel[u][:], sel_base[:], mask_term[:, bass.ds(b, 1), :].broadcast_to((128, 4, N)), ALU.add)\
                    .then_inc(s["c_sel"], 1)
                p.tensor_copy(nm[u][:, :, MROW], valid[:, bass.ds(b, 1)].broadcast_to((N, 4))).then_inc(s["c_nv"], 1)

            def lower(b, u):
                for n, (hi, lo, signal) in enumerate(((slice(0, 2), slice(2, 4), "c_hiq"),
                                                      (slice(0, 4, 2), slice(1, 4, 2), "c_hik"))):
                    pool.wait_ge(s[signal], b + 1)
                    p.tensor_tensor(qkx[u][:, n, :, lo].bitcast(F32R), qk[u][:, n].unsqueeze(2).broadcast_to((N, H, 2, HD)),
                                    qkx[u][:, n, :, hi], ALU.subtract).then_inc(s["c_lo"], 1)

            def residual(b, u):
                pool.wait_ge(s["c_at"], b + 1)
                settled(pool)
                p.tensor_tensor(gated[u][:], attn[u][:], gate[:, bass.ds(b, 1), 0, :].rearrange("p a c -> p (a c)"), ALU.mult)\
                    .then_inc(s["c_ga"], 1)
                pool.wait_ge(s["c_ga"], b + 1)
                pool.wait_ge(s["c_xb"], b + 1)
                settled(pool)
                p.tensor_tensor(batch(xs, b), gated[u][:], batch(xb, b), ALU.add).then_inc(s["c_res"], 1)

            def step(b, u, end=True, front=True, ahead=True):
                if front:
                    lower(b + 1, 1 - u)
                if end:
                    residual(b - 2, u)
                if ahead:
                    prepare(b + 2, u)

            pool.wait_ge(s["mterm_ok"], 1)
            pool.wait_ge(s["selbase_ok"], 1)
            pool.wait_ge(s["gate_in"], 16)
            pool.wait_ge(s["pbias_ok"], 1)
            pool.wait_ge(s["valid_ok"], 1)
            pool.wait_ge(s["c_vinit"], 10)
            pool.wait_ge(s["maskb_ok"], 1)
            prepare(0, 0)
            root(2, 1, s["c_pow"])
            prepare(1, 1)
            lower(0, 0)
            root(2, 2, s["c_pow"])
            root(2, 3, s["c_pow"])
            step(0, 0, end=False)
            step(1, 1, end=False)
            with pool.Fori(0, B // 2 - 2) as i:
                step(2 * i + 2, 0)
                step(2 * i + 3, 1)
            step(B - 2, 0, ahead=False)

            def d_bias(g):
                b = G * g
                p.tensor_tensor(gtmp[:], gate[:, b:b + G, 1, :], row("fc2_b").unsqueeze(1).broadcast_to((N, G, C)),
                                ALU.mult).then_inc(s["d_gp"], 1)
                pool.wait_ge(s["d_gp"], g + 1)
                p.tensor_tensor(xb[:, b:b + G], xs[:, b:b + G], gtmp[:], ALU.add).then_inc(s["d_xb"], 1)
                pool.wait_ge(s["d_xb"], g + 1)

            root(3, 0, s["d_pow"])
            root(3, 1, s["d_pow"])
            root(3, 2, s["d_pow"])
            step(B - 1, 1, front=False, ahead=False)
            residual(B - 2, 0)
            residual(B - 1, 1)
            pool.wait_ge(s["c_res"], B)
            d_bias(0)
            root(3, 3, s["d_pow"])
            for g in range(1, 4):
                d_bias(g)


def kernel(**inputs):
    import numpy as np
    import concourse.bacc as bacc
    from concourse.bass_utils import run_bass_kernel_spmd

    a = {k: np.asarray(v) for k, v in inputs.items()}
    l0 = {k[8:]: v for k, v in a.items() if k.startswith("L0_cond_")}
    l1 = {k[8:]: v for k, v in a.items() if k.startswith("L1_cond_")}

    def columns(*vectors):
        cols = np.concatenate([v.reshape(-1, 128) for v in vectors]).T
        return np.concatenate([cols, np.zeros((128, 16 - cols.shape[1]), np.float32)], axis=1)

    packed = {
        "cond": a["cond_1024"].T, "film1": l0["film1_w"], "film2": l0["film2_w"],
        "cols0": columns(l0["q_b"], l0["k_b"], l0["v_b"], l0["norm1_w"], l0["norm2_w"], l0["film1_b"],
                         l0["film2_b"], l0["mlp_b1"]),
        "q": l0["q_w"], "k": l0["k_w"], "vt": l0["v_w"].T, "proj": l0["proj_w"], "mlp1": l0["mlp_w1"],
        "mlp2": l0["mlp_w2"].reshape(FC, 128, C).transpose(1, 0, 2).reshape(128, F),
        "ada": l1["ada_w"].T,
        "cols1": columns(l1["ada_b"], l1["qkv_b"][2 * C:], l1["fc1_b"]),
        "qkv": l1["qkv_w"].T,
        "proj1": l1["proj_w"].T, "fc1": l1["fc1_w"].T,
        "fc2": l1["fc2_w"].T.reshape(FC, 128, C).transpose(1, 0, 2).reshape(128, F),
    }
    ada_b = l1["ada_b"].reshape(6, C)
    in_map = {
        "x": np.ascontiguousarray(a["x"].transpose(1, 0, 2)),
        "weights": np.ascontiguousarray(np.concatenate([packed[n] for n, size in _W if size], axis=1)),
        "rows": np.concatenate([l0["proj_b"], l0["mlp_b2"], l1["qkv_b"][:2 * C], l1["proj_b"], l1["fc2_b"],
                                ada_b[2], ada_b[5]]),
        "mask": a["mask_BxS_bk1"].astype(np.int32),
        "mask_t": np.ascontiguousarray(a["mask_BxS_bk1"].T).astype(np.int32),
    }
    nc = bacc.Bacc("TRN2", target_bir_lowering=False, num_devices=1)
    aps = [nc.dram_tensor(n, v.shape, mybir.dt.from_np(v.dtype), kind="ExternalInput").ap() for n, v in in_map.items()]
    gates = nc.dram_tensor("gates", (B, 2 * C), F32, kind="Internal").ap()
    out = nc.dram_tensor("out", (N, B, C), F32, kind="ExternalOutput").ap()
    build(nc, *aps, gates, out)
    result = run_bass_kernel_spmd(nc, [in_map], core_ids=[0])
    return np.ascontiguousarray(result.results[0]["out"].transpose(1, 0, 2))
```

```python
from contextlib import ExitStack

import concourse.bass as bass
from concourse import mybir

F32 = mybir.dt.float32
F32R = mybir.dt.float32r
BF16 = mybir.dt.bfloat16
I32 = mybir.dt.int32
ALU = mybir.AluOpType
ACT = mybir.ActivationFunctionType
AX = mybir.AxisListType

B, N, C = 16, 128, 128
H, HD = 16, 8
F = 4 * C
FC = F // C
G = 4
EPS = 1e-6
MASKED = -1e9
ROWS = 32
MROW = 16

_W = [("cond", B), ("film1", 2 * C), ("film2", 2 * C), ("cols0", 16), ("q", C), ("k", C), ("vt", C),
      ("proj", C), ("x_end", 0), ("mlp1", F), ("mlp2", F), ("m_end", 0), ("ada", 6 * C),
      ("cols1", 16), ("qkv", 3 * C), ("proj1", C), ("fc1", F), ("fc2", F)]
W_AT, _n = {}, 0
for _name, _size in _W:
    W_AT[_name] = _n
    _n += _size
W_ALL = _n
_R = [("proj_b", C), ("mlp_b2", C), ("qk_b", 2 * C), ("proj1_b", C), ("fc2_b", C), ("gate_b", 2 * C)]
R_AT, _n = {}, 0
for _name, _size in _R:
    R_AT[_name] = _n
    _n += _size
R_ALL = _n


def build(nc, x, weights, rows, mask, mask_t, gates, out):
    with ExitStack() as ctx:
        def sb(name, shape, dt=F32):
            return ctx.enter_context(nc.sbuf_tensor(name, shape, dt))

        def sem(name):
            return ctx.enter_context(nc.semaphore(name))

        W = sb("W", [128, W_ALL])
        R = sb("R", [128, R_ALL])
        xs = sb("xs", [N, B, C])
        xb = sb("xb", [N, B, C])
        agg = sb("agg", [N, G, 2])
        mean = sb("mean", [N, 2, B])
        rstd = sb("rstd", [N, 4, B])
        var_eps = sb("var_eps", [N, 4, B])
        mean_sq = sb("mean_sq", [N, G])
        bn = sb("bn", [N, G, 6])
        bn_c = sb("bn_c", [N, 6])
        agg_c = sb("agg_c", [N, 2])
        half = sb("half", [N, B])
        ident = sb("ident", [128, 128])
        xn = [sb(f"xn{u}", [N, G, C]) for u in range(2)]
        hT = [sb(f"hT{u}", [C, G, N]) for u in range(2)]
        scale = sb("scale", [C, 4, B])
        shift = sb("shift", [C, 4, B])
        shared = sb("shared", [128, 8, G, N])
        qT, kT, v0, p0 = ([shared[:, 2 * n + u] for u in range(2)] for n in range(4))
        pT0 = [sb(f"apT{u}", [N, G, N]) for u in range(2)]
        amax = sb("amax", [N, 2, G])
        aden = sb("aden", [N, 2, G])
        arden = sb("arden", [N, 2, G])
        wvp = sb("wvp", [C, C])
        bias_a = sb("bias_a", [N, C])
        bcol = sb("bcol", [C, N])
        hid = [sb(f"hid{u}", [128, FC, G, N]) for u in range(2)]
        gmul = [sb(f"gmul{u}", [N, G, C]) for u in range(2)]
        cond_e = sb("cond_e", [C, B])
        cond_s = sb("cond_s", [C, B])
        cond_r = sb("cond_r", [C, B])
        silu = sb("silu", [C, B])
        gate_rows = sb("gate_rows", [B, 2, C])
        gate = sb("gate", [N, B, 2, C])
        pbias1 = sb("pbias1", [N, C])
        bcol1 = sb("bcol1", [C, N])
        gtmp = sb("gtmp", [N, G, C])
        mask_i = sb("mask_i", [128, B, N], I32)
        maskt_i = sb("maskt_i", [N, B], I32)
        valid = sb("valid", [N, B])
        mod32 = sb("mod32", [128, 32])
        sel_f = sb("sel_f", [128, 4])
        row_mask = sb("row_mask", [128, 1])
        quarter = sb("quarter", [128, 1])
        row_amp = sb("row_amp", [128, 1])
        row_neg = sb("row_neg", [128, 1])
        mask_rows = sb("mask_rows", [128, N], I32)
        mask_term = sb("mask_term", [128, N])
        sel = sb("sel", [128, 4, N], F32R)
        spare = sb("spare", [N, 1])
        eye = sb("eye", [N, B, B])
        own = sb("own", [N, B, B])
        upto = sb("upto", [128, 128])
        mask_b = sb("mask_b", [128, B, N], BF16)
        first = sb("first", [N, B])
        nofirst = [sb(f"nofirst{u}", [N, N]) for u in range(2)]
        keep = [sb(f"keep{u}", [N, N]) for u in range(2)]
        turn_k = [sb(f"turn_k{u}", [N, N], F32R) for u in range(2)]
        xc = [sb(f"xc{u}", [N, C]) for u in range(2)]
        hc = [sb(f"hc{u}", [C, N]) for u in range(2)]
        qbv = [sb(f"qbv{u}", [N, C]) for u in range(2)]
        qk = [sb(f"qk{u}", [N, 2, H, HD]) for u in range(2)]
        qkx = [sb(f"qkx{u}", [N, 2, H, 4, HD]) for u in range(2)]
        qxT = [sb(f"qxT{u}", [128, 4, N], F32R) for u in range(2)]
        kxT = [sb(f"kxT{u}", [128, 4, N], F32R) for u in range(2)]
        qdiag = [sb(f"qdiag{u}", [128, 4, 4, N], F32R) for u in range(2)]
        kdiag = [sb(f"kdiag{u}", [128, 4, 4, N], F32R) for u in range(2)]
        vx = [sb(f"vx{u}", [N, 8 * 64]) for u in range(2)]
        nmax = [sb(f"nmax{u}", [N, 16]) for u in range(2)]
        nm = [sb(f"nm{u}", [N, 4, 32]) for u in range(2)]
        nmdiag = [sb(f"nmdiag{u}", [128, 4, N], F32R) for u in range(2)]
        pT = [shared[:, 4 * u:4 * u + 4] for u in range(2)]
        oT = [sb(f"oT{u}", [128, 2, N]) for u in range(2)]
        rden = [sb(f"rden{u}", [N, 16]) for u in range(2)]
        on = [sb(f"on{u}", [N, 16, HD]) for u in range(2)]
        onT = [sb(f"onT{u}", [C, N]) for u in range(2)]
        attn = [sb(f"attn{u}", [N, C]) for u in range(2)]
        gated = [sb(f"gated{u}", [N, C]) for u in range(2)]

        ps = ctx.enter_context(nc.psum_tensor("ps", [128, 8, 512], F32))

        def bank(i):
            return ps[:, i, :].rearrange("p (g n) -> p g n", g=G)

        def w(name, size=C, at=0):
            a = W_AT[name] + at
            return W[:, a:a + size]

        def row(name, size=C, at=0):
            a = R_AT[name] + at
            return R[:, a:a + size]

        def col(name, j):
            return w(name, 1, j)

        COL = {"q_b": 0, "k_b": 1, "v_b": 2, "n1": 3, "n2": 4, "film1": 5, "film2": 7, "mlp_b1": 9}
        COL1 = {"ada": 0, "v_b": 6, "fc1": 7}

        names = """settled x_in0 x_in1 x_in2 x_in3 w_film w_attn0 w_ada w_mlp0 w_block1 rows_in mask_in gate_out gate_in y_out
            ident_ok half_ok spare_ok stats_ok film_mm film_one film_ok silu_e silu_one silu_ok
            ada_mm ada_ok gate_ok bias_mm wvp_mm wvp_ok bias_ok bcol_ok pbias_ok
            valid_ok mod32_ok selc_ok mterm_ok sel_ok eye_ok own_ok rows_ok mask_rows_in upto_ok maskb_ok diag_ok
            c_first c_keep c_turn c_vinit
            a_pow a_xn a_xb a_T a_h a_Q a_K a_V a_qT a_kT a_v a_S a_max a_exp a_PT a_pT a_PV a_rden a_res
            b_pow b_xn b_xb b_T b_h b_M1 b_gelu b_M2 b_res
            c_pow c_xb c_gp c_nv c_qbv c_xc c_Tx c_h c_QK c_V c_q c_k c_v c_hiq c_hik c_lo c_Tq c_Tk c_qT c_kT c_qd c_kd c_kd3
            c_S c_max c_nm c_NT c_nmT c_ST c_exp c_PV c_oT c_T2 c_rden c_on c_T3 c_onT c_pr c_at c_ga c_res c_st
            d_pow d_xn d_xb d_T d_h d_M1 d_gelu d_M2 d_gm d_gp d_res""".split()
        s = {n: sem(n) for n in names}

        PER_GROUP = 2 * G + 2

        def stats_end(k, g):
            return PER_GROUP * (G * k + g + 1)

        def settled(eng):
            eng.sem_inc(s["settled"], 1)

        def batch(t, b):
            return t[:, bass.ds(b, 1), :].rearrange("p a c -> p (a c)")

        block = ctx.enter_context(nc.Block())

        @block.sync
        def _(sp):
            sp.dma_start(xs[:, 0:G], x[:, 0:G]).then_inc(s["x_in0"], 16)
            for n, (a, b) in enumerate((("q", "x_end"), ("ada", "qkv"), ("mlp1", "m_end"), ("qkv", None))):
                a, b = W_AT[a], W_AT[b] if b else W_ALL
                sp.dma_start(W[:, a:b], weights[:, a:b]).then_inc(s[("w_attn0", "w_ada", "w_mlp0", "w_block1")[n]], 16)
                if n == 0:
                    for g in range(1, 4):
                        sp.dma_start(xs[:, G * g:G * g + G], x[:, G * g:G * g + G]).then_inc(s[f"x_in{g}"], 16)
            sp.wait_ge(s["rows_ok"], 1)
            for r in range(4):
                sp.dma_start(mask_rows[32 * r + MROW:32 * r + 32, :], mask).then_inc(s["mask_rows_in"], 16)
            sp.wait_ge(s["gate_ok"], 1)
            sp.dma_start(gates, gate_rows[:].rearrange("b g c -> b (g c)")).then_inc(s["gate_out"], 16)
            sp.wait_ge(s["gate_out"], 16)
            sp.dma_start(gate[:], gates.rearrange("b f -> (b f)").partition_broadcast(128)).then_inc(s["gate_in"], 16)
            for n, (b, size) in enumerate(((0, G), (G, G), (2 * G, G), (3 * G, 2), (3 * G + 2, 2))):
                sp.wait_ge(s["d_res"], n + 1)
                sp.dma_start(out[:, b:b + size], xs[:, b:b + size]).then_inc(s["y_out"], 16)
            sp.wait_ge(s["y_out"], 5 * 16)

        @block.tensor
        def _(pe):
            mm = nc.tensor.matmul

            def transposes(dst, src, signal):
                for j in range(G):
                    ins = nc.tensor.transpose(dst[:, j], src[:, j], ident[:])
                ins.then_inc(signal, 1)

            def a_norm(g):
                pe.wait_ge(s["a_xn"], g + 1)
                transposes(bank(0), xn[g % 2], s["a_T"])

            def a_qk(g, n):
                if n == 0:
                    pe.wait_ge(s["a_h"], g + 1)
                mm(ps[:, 1 + n, :], w("qk"[n]), hT[g % 2][:], start=True, stop=True).then_inc(s[("a_Q", "a_K")[n]], 1)

            def a_value(g):
                pe.wait_ge(s["wvp_ok"], 1)
                for j in range(G):
                    ins = mm(bank(3)[:, j], hT[g % 2][:, j], wvp[:], start=True, stop=True, skip_group_check=True)
                ins.then_inc(s["a_V"], 1)

            def a_scores(g):
                u = g % 2
                pe.wait_ge(s["a_qT"], g + 1)
                pe.wait_ge(s["a_kT"], g + 1)
                for j in range(G):
                    ins = mm(bank(4 + 3 * u)[:, j], qT[u][:, j], kT[u][:, j], start=True, stop=True, skip_group_check=True)
                ins.then_inc(s["a_S"], 1)
                pe.wait_ge(s["a_v"], g + 1)

            def a_turn(g):
                pe.wait_ge(s["a_exp"], G * (g + 1))
                transposes(bank(5), p0[g % 2], s["a_PT"])

            def a_weighted(g):
                pe.wait_ge(s["a_pT"], g + 1)
                if g:
                    pe.wait_ge(s["a_res"], G * g)
                for j in range(G):
                    ins = mm(bank(6)[:, j], pT0[g % 2][:, j], v0[g % 2][:, j], start=True, stop=True, skip_group_check=True)
                ins.then_inc(s["a_PV"], 1)

            def m_norm(p, g, t_bank):
                pe.wait_ge(s[p + "xn"], g + 1)
                if g:
                    pe.wait_ge(s[p + "h"], g)
                transposes(bank(t_bank), xn[g % 2], s[p + "T"])

            def m_up(p, g, w1, h_bank, chunks=range(FC)):
                for f in chunks:
                    if f == 0:
                        pe.wait_ge(s[p + "h"], g + 1)
                    if g:
                        pe.wait_ge(s[p + "gelu"], FC * (g - 1) + f + 1)
                    mm(ps[:, h_bank + f, :], w(w1, C, C * f), hT[g % 2][:], start=True, stop=True).then_inc(s[p + "M1"], 1)

            def m_down(p, g, w2, o_bank, js=range(G)):
                pe.wait_ge(s[p + "gelu"], FC * (g + 1))
                if p == "b_" and g:
                    pe.wait_ge(s["b_res"], g)
                if p == "d_" and g > 1:
                    pe.wait_ge(s["d_gm"], g - 1)
                for j in js:
                    for f in range(FC):
                        ins = mm(bank(o_bank)[:, j], hid[g % 2][:, f, j], w(w2, C, C * f),
                                 start=(f == 0), stop=(f == FC - 1), skip_group_check=True)
                    if j == G - 1 or (p == "d_" and j == G // 2 - 1):
                        ins.then_inc(s[p + "M2"], 1)

            def front_a(b, u, at=(7, C)):
                pe.wait_ge(s["c_xc"], b + 1)
                nc.tensor.transpose(ps[:, at[0], at[1]:at[1] + N], xc[u][:], ident[:]).then_inc(s["c_Tx"], 1)

            def front_b(b, u):
                pe.wait_ge(s["c_h"], b + 1)
                mm(ps[:, 4, 0:2 * C], hc[u][:], w("qkv", 2 * C), start=True, stop=True).then_inc(s["c_QK"], 1)
                if not isinstance(b, int) or b:
                    pe.wait_ge(s["c_kT"], b)
                mm(ps[:, 7, 0:C], hc[u][:], w("qkv", C, 2 * C), start=True, stop=True).then_inc(s["c_V"], 1)

            def split_rows(u, n, t):
                return qkx[u][:, n].rearrange("n (t r) s d -> n t (r s d)", t=4)[:, t]

            def front_q(b, u):
                pe.wait_ge(s["c_lo"], 2 * b + 1)
                for t in range(4):
                    ins = nc.tensor.transpose(bank(6)[:, t], split_rows(u, 0, t), ident[:])
                ins.then_inc(s["c_Tq"], 1)

            def front_k(b, u):
                pe.wait_ge(s["c_lo"], 2 * b + 2)
                pe.wait_ge(s["c_turn"], b + 1)
                pe.wait_ge(s["c_v"], b + 1)
                for t in range(4):
                    ins = mm(bank(7)[:, t], split_rows(u, 1, t).bitcast(F32R), turn_k[u][:], start=True, stop=True,
                             skip_group_check=True)
                ins.then_inc(s["c_Tk"], 1)

            def scores(b, u, halves, back):
                if 0 in halves:
                    pe.wait_ge(s["c_qT"], b + 1)
                    pe.wait_ge(s["c_kd"], b + 1)
                    pe.wait_ge(s["c_kd3"], b + 1)
                for t in (t for e in halves for t in (2 * e, 2 * e + 1)):
                    if back and t % 2 == 0:
                        pe.wait_ge(s["c_exp"], 2 * b + t // 2 - 1)
                    ins = mm(ps[:, t, :], qxT[u][:, t], kdiag[u][:, t], start=True, stop=True)
                    if t % 2:
                        ins.then_inc(s["c_S"], 1)

            def scores_t(b, u, e):
                if e == 0:
                    pe.wait_ge(s["c_kT"], b + 1)
                    pe.wait_ge(s["c_qd"], 3 * b + 3)
                pe.wait_ge(s["c_max"], 2 * b + e + 1)
                for t in (2 * e, 2 * e + 1):
                    mm(ps[:, t, :], kxT[u][:, t], qdiag[u][:, t], start=True, stop=False, skip_group_check=True)

            def turn_maxima(b, u):
                pe.wait_ge(s["c_nm"], 2 * b + 2)
                pe.wait_ge(s["c_nv"], b + 1)
                nc.tensor.transpose(ps[:, 4, 256:256 + N], nm[u][:].rearrange("n r k -> n (r k)"), ident[:])\
                    .then_inc(s["c_NT"], 1)

            def subtract_maxima(b, u):
                for e in range(2):
                    pe.wait_ge(s["c_nmT"], 2 * b + e + 1)
                    for t in range(4):
                        ins = mm(bank(t)[:, 2 * e:2 * e + 2], sel[:, t], nmdiag[u][:, 2 * e:2 * e + 2], start=False,
                                 stop=True, skip_group_check=True)
                        if e and t % 2:
                            ins.then_inc(s["c_ST"], 1)

            def weighted(b, u, e):
                pe.wait_ge(s["c_exp"], 2 * b + e + 1)
                if e == 0:
                    pe.wait_ge(s["c_v"], b + 1)
                    if not isinstance(b, int) or b:
                        pe.wait_ge(s["c_on"], b)
                    else:
                        pe.wait_ge(s["b_res"], 4)
                v = vx[u][:].rearrange("n (e j s c) -> n e j s c", e=2, j=4, s=2)
                p = pT[u].rearrange("n (e t) (k s) q -> n e (t k) s q", e=2, k=2)
                for s2 in range(2):
                    for j in range(4):
                        ins = mm(ps[32 * j:32 * j + 32, 5, N * e:N * e + N], v[:, e, j, s2], p[:, e, j, s2],
                                 start=(s2 == 0), stop=(s2 == 1), skip_group_check=True)
                ins.then_inc(s["c_PV"], 1)

            def back_a(b, u):
                pe.wait_ge(s["c_oT"], b + 1)
                for e in range(2):
                    ins = nc.tensor.transpose(ps[:, 5, 128 * e:128 * e + 128], oT[u][:, e], ident[:])
                ins.then_inc(s["c_T2"], 1)

            def back_b(b, u, t_bank=6):
                pe.wait_ge(s["c_on"], b + 1)
                nc.tensor.transpose(ps[:, t_bank, 0:N], on[u][:].rearrange("n h d -> n (h d)"), ident[:]).then_inc(s["c_T3"], 1)

            def back_c(b, u, bank=6):
                pe.wait_ge(s["c_onT"], b + 1)
                mm(ps[:, bank, 2 * N:2 * N + C], onT[u][:], w("proj1"), start=True, stop=True).then_inc(s["c_pr"], 1)

            def step(b, u, end=True, back=True, front=True, ahead=True):
                scores(b, u, (0,), back)
                if ahead:
                    front_a(b + 2, u)
                scores(b, u, (1,), back)
                if end:
                    back_b(b - 2, u)
                if not back:
                    m_down("b_", 3, "mlp2", 5, range(2, 4))
                if back:
                    weighted(b - 1, 1 - u, 0)
                if end:
                    back_c(b - 2, u)
                if back:
                    weighted(b - 1, 1 - u, 1)
                if end:
                    pe.wait_ge(s["c_at"], b - 1)
                if front:
                    front_q(b + 1, 1 - u)
                else:
                    m_norm("d_", 0, 6)
                scores_t(b, u, 0)
                if front:
                    pe.wait_ge(s["c_k"], b + 2)
                turn_maxima(b, u)
                scores_t(b, u, 1)
                if front:
                    front_k(b + 1, 1 - u)
                if back:
                    back_a(b - 1, 1 - u)
                subtract_maxima(b, u)
                if ahead:
                    front_b(b + 2, u)

            pe.wait_ge(s["w_film"], 16)
            for j in range(4):
                ins = mm(ps[:, 7, B * j:B * j + B], w(("film1", "film2")[j // 2], C, C * (j % 2)), w("cond", B),
                         start=(j == 0), stop=True, skip_group_check=True)
            ins.then_inc(s["film_mm"], 1)
            pe.wait_ge(s["ident_ok"], 2)
            a_norm(0)
            pe.wait_ge(s["w_attn0"], 16)
            mm(ps[:, 6, 0:C], w("vt"), w("proj"), start=True, stop=True).then_inc(s["wvp_mm"], 1)
            pe.wait_ge(s["bcol_ok"], 1)
            mm(ps[:, 5, 0:C], bcol[:], w("proj"), start=True, stop=True).then_inc(s["wvp_mm"], 1)
            a_qk(0, 0)
            a_norm(1)
            a_qk(0, 1)
            a_value(0)
            a_scores(0)
            for g in range(3):
                a_qk(g + 1, 0)
                a_qk(g + 1, 1)
                a_value(g + 1)
                if g < 2:
                    a_norm(g + 2)
                if g == 0:
                    pe.wait_ge(s["bias_ok"], 1)
                a_turn(g)
                if g == 2:
                    m_norm("b_", 0, 4)
                a_scores(g + 1)
                a_weighted(g)
            pe.wait_ge(s["w_mlp0"], 16)
            m_up("b_", 0, "mlp1", 0)
            a_turn(3)
            m_norm("b_", 1, 4)
            a_weighted(3)
            pe.wait_ge(s["w_ada"], 16)
            pe.wait_ge(s["silu_ok"], 1)
            for n, j in enumerate((1, 4, 0, 3)):
                ins = mm(ps[:, 7, B * n:B * n + B], w("ada", C, C * j), silu[:], start=(n == 0), stop=True,
                         skip_group_check=True)
            pe.wait_ge(s["upto_ok"], 2)
            pe.wait_ge(s["valid_ok"], 1)
            ins = mm(ps[:, 7, 4 * B:5 * B], upto[:], valid[:], start=False, stop=True, skip_group_check=True)
            for n, j in enumerate((2, 5)):
                ins = mm(ps[0:B, 7, C * n + C:C * n + 2 * C], silu[:], w("ada", C, C * j), start=False, stop=True,
                         skip_group_check=True)
            ins.then_inc(s["ada_mm"], 1)
            m_up("b_", 1, "mlp1", 0)
            pe.wait_ge(s["a_res"], B)
            pe.wait_ge(s["w_block1"], 16)
            pe.wait_ge(s["bcol_ok"], 2)
            mm(ps[:, 6, 0:C], bcol1[:], w("proj1"), start=True, stop=True).then_inc(s["bias_mm"], 1)
            m_norm("b_", 2, 4)
            m_down("b_", 0, "mlp2", 5)
            m_up("b_", 2, "mlp1", 0)
            m_norm("b_", 3, 4)
            m_down("b_", 1, "mlp2", 5)
            pe.wait_ge(s["pbias_ok"], 1)
            front_a(0, 0, (6, 0))
            m_up("b_", 3, "mlp1", 0)
            pe.wait_ge(s["gate_ok"], 1)
            front_b(0, 0)
            front_a(1, 1, (6, 0))
            m_down("b_", 2, "mlp2", 5)
            pe.wait_ge(s["c_h"], 2)
            front_q(0, 0)
            front_k(0, 0)
            pe.wait_ge(s["c_k"], 1)
            front_b(1, 1)
            m_down("b_", 3, "mlp2", 5, range(2))
            pe.wait_ge(s["c_vinit"], 10)
            pe.wait_ge(s["sel_ok"], 1)
            step(0, 0, end=False, back=False)
            step(1, 1, end=False)
            with pe.Fori(0, B // 2 - 3) as i:
                step(2 * i + 2, 0)
                step(2 * i + 3, 1)
            step(B - 4, 0)
            step(B - 3, 1)
            step(B - 2, 0, ahead=False)
            step(B - 1, 1, front=False, ahead=False)

            back_b(B - 2, 0, 4)
            m_norm("d_", 1, 6)
            pe.wait_ge(s["c_exp"], 2 * B - 1)
            m_up("d_", 0, "fc1", 0, range(2))
            back_c(B - 2, 0, 4)
            weighted(B - 1, 1, 0)
            weighted(B - 1, 1, 1)
            m_up("d_", 0, "fc1", 0, range(2, 4))
            back_a(B - 1, 1)
            m_up("d_", 1, "fc1", 0, range(2))
            back_b(B - 1, 1, 4)
            m_up("d_", 1, "fc1", 0, range(2, 4))
            back_c(B - 1, 1, 4)
            m_norm("d_", 2, 6)
            m_down("d_", 0, "fc2", 7)
            m_up("d_", 2, "fc1", 0)
            m_norm("d_", 3, 6)
            m_down("d_", 1, "fc2", 5)
            m_up("d_", 3, "fc1", 0)
            m_down("d_", 2, "fc2", 7)
            m_down("d_", 3, "fc2", 5, range(2))
            m_down("d_", 3, "fc2", 6, range(2, 4))

        @block.scalar
        def _(act):
            a = nc.scalar.activation
            act.dma_start(W[:, 0:W_AT["q"]], weights[:, 0:W_AT["q"]]).then_inc(s["w_film"], 16)
            act.dma_start(R[:, :], rows.partition_broadcast(128)).then_inc(s["rows_in"], 16)
            act.dma_start(mask_i[:], mask.rearrange("b n -> (b n)").partition_broadcast(128)).then_inc(s["mask_in"], 16)
            act.dma_start(maskt_i[:], mask_t).then_inc(s["mask_in"], 16)
            act.wait_ge(s["w_film"], 16)
            a(cond_e[:], w("cond", B), ACT.Exp, scale=-1.0).then_inc(s["silu_e"], 1)

            def affine(p, g, k, src):
                act.wait_ge(s[p + "T"], g + 1)
                for j in range(G):
                    b = G * g + j
                    ins = a(hT[g % 2][:, j], src[:, j], ACT.Identity, bias=shift[:, k, b:b + 1],
                            scale=scale[:, k, b:b + 1])
                ins.then_inc(s[p + "h"], 1)

            def a_kv(g):
                act.wait_ge(s["a_K"], g + 1)
                a(kT[g % 2][:], bank(2), ACT.Identity, bias=col("cols0", COL["k_b"])).then_inc(s["a_kT"], 1)
                act.wait_ge(s["a_V"], g + 1)
                a(v0[g % 2][:], bank(3), ACT.Copy).then_inc(s["a_v"], 1)

            def a_exp(g):
                u = g % 2
                act.wait_ge(s["a_max"], g + 1)
                for j in range(G):
                    a(p0[u][:, j], bank(4 + 3 * u)[:, j], ACT.Exp, bias=amax[:, u, j:j + 1],
                      accum_out=aden[:, u, j:j + 1]).then_inc(s["a_exp"], 1)

            act.wait_ge(s["film_ok"], 2)
            affine("a_", 0, 0, bank(0))
            act.wait_ge(s["wvp_mm"], 1)
            a(wvp[:], ps[:, 6, 0:C], ACT.Copy).then_inc(s["wvp_ok"], 1)
            affine("a_", 1, 0, bank(0))
            a_kv(0)
            a_exp(0)
            for g in range(1, 4):
                a_kv(g)
                if g < 3:
                    affine("a_", g + 1, 0, bank(0))
                else:
                    affine("b_", 0, 1, bank(4))
                a_exp(g)

            def gelus(p, g, func, bcols, bat, h_bank, chunks=range(FC)):
                for f in chunks:
                    act.wait_ge(s[p + "M1"], FC * g + f + 1)
                    if g > 1:
                        act.wait_ge(s[p + "M2"], (g - 1) * (2 if p == "d_" else 1))
                    a(hid[g % 2][:, f], bank(h_bank + f), func, bias=col(bcols, bat + f)).then_inc(s[p + "gelu"], 1)

            gelus("b_", 0, ACT.Gelu, "cols0", COL["mlp_b1"], 0)
            affine("b_", 1, 1, bank(4))
            gelus("b_", 1, ACT.Gelu, "cols0", COL["mlp_b1"], 0)
            affine("b_", 2, 1, bank(4))
            gelus("b_", 2, ACT.Gelu, "cols0", COL["mlp_b1"], 0)
            affine("b_", 3, 1, bank(4))

            def front_h(b, u, at=(7, C)):
                act.wait_ge(s["c_Tx"], b + 1)
                act.wait_ge(s["ada_ok"], 1)
                a(hc[u][:], ps[:, at[0], at[1]:at[1] + N], ACT.Identity, bias=shift[:, 2, bass.ds(b, 1)],
                  scale=scale[:, 2, bass.ds(b, 1)]).then_inc(s["c_h"], 1)

            def front_v(b, u):
                act.wait_ge(s["c_V"], b + 1)
                v = ps[:, 7, 0:C].rearrange("n (a k d) -> n a k d", k=2, d=HD)
                slots = vx[u][:].rearrange("n (a z) -> n a z", z=64)
                for k in range(2):
                    ins = a(slots[:, :, 48 * k:48 * k + HD], v[:, :, k], ACT.Copy)
                ins.then_inc(s["c_v"], 1)

            def front_hi(b, u):
                for n, (ready, slots, signal) in enumerate((("c_q", slice(0, 2), "c_hiq"), ("c_k", slice(0, 4, 2), "c_hik"))):
                    act.wait_ge(s[ready], b + 1)
                    a(qkx[u][:, n, :, slots].bitcast(F32R), qk[u][:, n].unsqueeze(2).broadcast_to((N, H, 2, HD)),
                      ACT.Copy).then_inc(s[signal], 1)

            def front_q(b, u):
                act.wait_ge(s["c_Tq"], b + 1)
                a(qxT[u][:], bank(6), ACT.Copy).then_inc(s["c_qT"], 1)

            def front_k(b, u):
                act.wait_ge(s["c_Tk"], b + 1)
                a(kxT[u][:], bank(7), ACT.Copy).then_inc(s["c_kT"], 1)

            def front_qdiag(b, u, rs):
                act.wait_ge(s["c_qT"], b + 1)
                for r in rs:
                    rows = slice(32 * r, 32 * r + 32)
                    ins = a(qdiag[u][rows, :, r], qxT[u][rows], ACT.Copy)
                ins.then_inc(s["c_qd"], 1)

            def weights_of(b, u, e):
                act.wait_ge(s["c_ST"], 2 * b + e + 1)
                a(pT[u][:, 2 * e:2 * e + 2], ps[:, 2 * e:2 * e + 2, :].rearrange("n t (r q) -> n t r q", r=4),
                  ACT.Exp, scale=HD ** -0.5).then_inc(s["c_exp"], 1)

            def turned_o(b, u, t_bank=6):
                act.wait_ge(s["c_T3"], b + 1)
                a(onT[u][:], ps[:, t_bank, 0:N], ACT.Copy).then_inc(s["c_onT"], 1)

            def back_o(b, u):
                act.wait_ge(s["c_PV"], 2 * b + 2)
                a(oT[u][:], ps[:, 5, 0:2 * N].rearrange("p (e n) -> p e n", e=2), ACT.Copy).then_inc(s["c_oT"], 1)

            def projected(b, u, bank=6):
                act.wait_ge(s["c_pr"], b + 1)
                a(attn[u][:], ps[:, bank, 2 * N:2 * N + C], ACT.Copy).then_inc(s["c_at"], 1)

            def step(b, u, end=True, back=True, front=True, ahead=True):
                if front:
                    front_hi(b + 1, 1 - u)
                if ahead:
                    front_h(b + 2, u)
                if end:
                    turned_o(b - 2, u)
                front_qdiag(b, u, (1, 2))
                if end:
                    projected(b - 2, u)
                front_qdiag(b, u, (3,))
                if back:
                    back_o(b - 1, 1 - u)
                if front:
                    front_v(b + 1, 1 - u)
                    front_q(b + 1, 1 - u)
                    front_qdiag(b + 1, 1 - u, (0,))
                    front_k(b + 1, 1 - u)
                else:
                    affine("d_", 0, 3, bank(6))
                weights_of(b, u, 0)
                weights_of(b, u, 1)

            front_h(0, 0, (6, 0))
            gelus("b_", 3, ACT.Gelu, "cols0", COL["mlp_b1"], 0)
            front_hi(0, 0)
            front_h(1, 1, (6, 0))
            act.wait_ge(s["c_vinit"], 6)
            front_v(0, 0)
            act.wait_ge(s["spare_ok"], 1)
            a(spare[:], spare[:], ACT.Exp)
            front_q(0, 0)
            front_k(0, 0)
            act.wait_ge(s["diag_ok"], 4)
            front_qdiag(0, 0, (0,))
            step(0, 0, end=False, back=False)
            step(1, 1, end=False)
            with act.Fori(0, B // 2 - 3) as i:
                step(2 * i + 2, 0)
                step(2 * i + 3, 1)
            step(B - 4, 0)
            step(B - 3, 1)
            step(B - 2, 0, ahead=False)
            step(B - 1, 1, front=False, ahead=False)
            turned_o(B - 2, 0, 4)
            gelu = ACT.Gelu_apprx_tanh
            gelus("d_", 0, gelu, "cols1", COL1["fc1"], 0, range(1))
            projected(B - 2, 0, 4)
            gelus("d_", 0, gelu, "cols1", COL1["fc1"], 0, range(1, 2))
            affine("d_", 1, 3, bank(6))
            back_o(B - 1, 1)
            gelus("d_", 0, gelu, "cols1", COL1["fc1"], 0, range(2, 4))
            gelus("d_", 1, gelu, "cols1", COL1["fc1"], 0)
            affine("d_", 2, 3, bank(6))
            gelus("d_", 2, gelu, "cols1", COL1["fc1"], 0)
            affine("d_", 3, 3, bank(6))
            gelus("d_", 3, gelu, "cols1", COL1["fc1"], 0)

        @block.vector
        def _(dve):
            v = nc.vector
            v.memset(half[:], -0.5).then_inc(s["half_ok"], 1)
            v.memset(spare[:], 0.0).then_inc(s["spare_ok"], 1)

            def statistics(k, g):
                ok = s["stats_ok"]
                base = stats_end(k, g) - PER_GROUP
                if base:
                    dve.wait_ge(ok, base)
                for j in range(G):
                    v.bn_stats(bn[:, j], xs[:, G * g + j]).then_inc(ok, 1)
                for j in range(G):
                    dve.wait_ge(ok, base + j + 1)
                    v.bn_aggr(agg[:, j], bn[:, j]).then_inc(ok, 1)
                ve = var_eps[:, k, G * g:G * g + G]
                dve.wait_ge(ok, base + 2 * G)
                if k < 2:
                    v.tensor_tensor(mean_sq[:], agg[:, :, 0], agg[:, :, 0], ALU.mult).then_inc(ok, 1)
                    dve.wait_ge(ok, base + 2 * G + 1)
                    v.scalar_tensor_tensor(out=ve, in0=agg[:, :, 1], scalar=EPS, in1=mean_sq[:], op0=ALU.add, op1=ALU.add)\
                        .then_inc(ok, 1)
                else:
                    v.tensor_copy(mean[:, 0, G * g:G * g + G], agg[:, :, 0]).then_inc(ok, 1)
                    v.tensor_scalar(ve, agg[:, :, 1], EPS, None, ALU.add).then_inc(ok, 1)

            def d_norm(g):
                dve.wait_ge(s["d_pow"], g + 1)
                if g > 1:
                    dve.wait_ge(s["d_T"], g - 1)
                for j in range(G):
                    b = G * g + j
                    ins = v.tensor_scalar(xn[g % 2][:, j], xs[:, b], mean[:, 1, b:b + 1], rstd[:, 3, b:b + 1],
                                          ALU.subtract, ALU.mult)
                ins.then_inc(s["d_xn"], 1)

            dve.wait_ge(s["x_in0"], 16)
            statistics(0, 0)
            dve.wait_ge(s["film_mm"], 1)
            for k, c in enumerate(("film1", "film2")):
                v.tensor_scalar(scale[:, k, :], ps[:, 7, 2 * B * k:2 * B * k + B], col("cols0", COL[c]), 1.0,
                                ALU.add, ALU.add).then_inc(s["film_one"], 1)
                v.tensor_scalar(shift[:, k, :], ps[:, 7, 2 * B * k + B:2 * B * k + 2 * B],
                                col("cols0", COL[c] + 1), None, ALU.add).then_inc(s["film_one"], 1)
            dve.wait_ge(s["film_one"], 4)
            for k, n in enumerate(("n1", "n2")):
                v.tensor_scalar(scale[:, k, :], scale[:, k, :], col("cols0", COL[n]), None, ALU.mult)\
                    .then_inc(s["film_ok"], 1)
            dve.wait_ge(s["x_in1"], 16)
            statistics(0, 1)
            dve.wait_ge(s["wvp_mm"], 2)
            dve.wait_ge(s["rows_in"], 16)
            v.tensor_tensor(bias_a[:], ps[:, 5, 0:C], row("proj_b"), ALU.add).then_inc(s["bias_ok"], 1)

            dve.wait_ge(s["ident_ok"], 2)
            v.tensor_reduce(mod32[:], ident[:].rearrange("p (r k) -> p k r", r=4), AX.X, ALU.add).then_inc(s["mod32_ok"], 1)
            dve.wait_ge(s["mod32_ok"], 1)
            v.tensor_reduce(sel_f[:], mod32[:, 0:8].rearrange("p (k t) -> p t k", t=4), AX.X, ALU.add)
            v.tensor_reduce(quarter[:], ident[:, 96:128], AX.X, ALU.add)
            v.tensor_reduce(row_mask[:], mod32[:, MROW:32], AX.X, ALU.add).then_inc(s["mod32_ok"], 1)
            dve.wait_ge(s["mod32_ok"], 2)
            v.tensor_scalar(row_amp[:], row_mask[:], -MASKED, None, ALU.mult)
            v.tensor_scalar(row_neg[:], row_mask[:], MASKED, None, ALU.mult).then_inc(s["selc_ok"], 1)
            dve.wait_ge(s["x_in2"], 16)
            statistics(0, 2)

            def a_q(g):
                dve.wait_ge(s["a_Q"], g + 1)
                v.tensor_scalar(qT[g % 2][:], bank(1), col("cols0", COL["q_b"]), C ** -0.5, ALU.add, ALU.mult)\
                    .then_inc(s["a_qT"], 1)

            def a_max(g):
                u = g % 2
                dve.wait_ge(s["a_S"], g + 1)
                v.tensor_reduce(amax[:, u, :], bank(4 + 3 * u), AX.X, ALU.max, negate=True).then_inc(s["a_max"], 1)

            def a_turn(g):
                dve.wait_ge(s["a_PT"], g + 1)
                v.tensor_copy(pT0[g % 2][:], bank(5)).then_inc(s["a_pT"], 1)

            def a_residual(g):
                u = g % 2
                dve.wait_ge(s["a_exp"], G * (g + 1))
                v.reciprocal(arden[:, u, :], aden[:, u, :]).then_inc(s["a_rden"], 1)
                dve.wait_ge(s["a_rden"], g + 1)
                dve.wait_ge(s["a_xb"], g + 1)
                dve.wait_ge(s["a_PV"], g + 1)
                for j in range(G):
                    b = G * g + j
                    v.scalar_tensor_tensor(out=xs[:, b], in0=bank(6)[:, j], scalar=arden[:, u, j:j + 1], in1=xb[:, b],
                                           op0=ALU.mult, op1=ALU.add).then_inc(s["a_res"], 1)

            a_q(0)
            dve.wait_ge(s["x_in3"], 16)
            statistics(0, 3)
            a_max(0)
            dve.wait_ge(s["mask_in"], 32)
            v.tensor_copy(valid[:], maskt_i[:]).then_inc(s["valid_ok"], 1)
            for g in range(4):
                if g < 3:
                    a_q(g + 1)
                elif g == 3:
                    statistics(1, 2)
                a_turn(g)
                if g in (1, 2):
                    statistics(1, g - 1)
                if g < 3:
                    a_max(g + 1)
                a_residual(g)
                dve.wait_ge(s["a_res"], G * (g + 1))
                if g == 0:
                    dve.wait_ge(s["silu_e"], 1)
                    v.tensor_scalar(cond_s[:], cond_e[:], 1.0, None, ALU.add).then_inc(s["silu_one"], 1)
                    dve.wait_ge(s["silu_one"], 1)
                    v.reciprocal(cond_r[:], cond_s[:]).then_inc(s["silu_one"], 1)
                    dve.wait_ge(s["silu_one"], 2)
                    v.tensor_tensor(silu[:], w("cond", B), cond_r[:], ALU.mult).then_inc(s["silu_ok"], 1)

            statistics(1, 3)

            def b_residual(g):
                b = G * g
                dve.wait_ge(s["b_M2"], g + 1)
                dve.wait_ge(s["b_xb"], g + 1)
                v.tensor_tensor(xs[:, b:b + G], bank(5), xb[:, b:b + G], ALU.add).then_inc(s["b_res"], 1)
                dve.wait_ge(s["b_res"], g + 1)
                statistics(2, g)

            def d_residual(g, j, n):
                b = G * g + j
                dve.wait_ge(s["d_M2"], 2 * g + (j + n) // 2)
                rows = slice(j, j + n)
                o = bank(6 if n < G and j else (7, 5)[g % 2])[:, rows]
                v.tensor_tensor(gmul[g % 2][:, rows], o, gate[:, b:b + n, 1, :], ALU.mult).then_inc(s["d_gm"], 1)
                dve.wait_ge(s["d_gm"], g + 1 + j // 2)
                dve.wait_ge(s["d_xb"], g + 1)
                v.tensor_tensor(xs[:, b:b + n], gmul[g % 2][:, rows], xb[:, b:b + n], ALU.add).then_inc(s["d_res"], 1)

            dve.wait_ge(s["valid_ok"], 1)
            dve.wait_ge(s["ada_mm"], 1)
            v.scalar_tensor_tensor(out=first[:], in0=ps[:, 7, 4 * B:5 * B], scalar=1.0, in1=valid[:], op0=ALU.is_equal,
                                   op1=ALU.mult)
            for n, j in enumerate((1, 4, 0, 3)):
                dst = scale[:, 2 + n, :] if n < 2 else shift[:, n, :]
                ins = v.tensor_scalar(dst, ps[:, 7, B * n:B * n + B], col("cols1", COL1["ada"] + j),
                                      1.0 if n < 2 else 0.0, ALU.add, ALU.add)
            ins.then_inc(s["ada_ok"], 1)
            v.tensor_tensor(gate_rows[:].rearrange("b g c -> b (g c)"), ps[0:B, 7, C:3 * C], row("gate_b", 2 * C)[0:B, :],
                            ALU.add).then_inc(s["gate_ok"], 1)
            dve.wait_ge(s["bias_mm"], 1)
            v.tensor_tensor(pbias1[:], ps[:, 6, 0:C], row("proj1_b"), ALU.add).then_inc(s["pbias_ok"], 1)
            b_residual(0)

            def front_x(b, u):
                if not isinstance(b, int) or b >= 2:
                    dve.wait_ge(s["c_Tx"], b - 1)
                v.tensor_scalar(xc[u][:], batch(xs, b), mean[:, 0, bass.ds(b, 1)], rstd[:, 2, bass.ds(b, 1)],
                                ALU.subtract, ALU.mult).then_inc(s["c_xc"], 1)

            def front_qk(b, u):
                dve.wait_ge(s["c_QK"], b + 1)
                dve.wait_ge(s["c_qbv"], b + 1)
                v.scalar_tensor_tensor(out=qk[u][:, 0].rearrange("n h d -> n (h d)"), in0=ps[:, 4, 0:C],
                                       scalar=valid[:, bass.ds(b, 1)], in1=qbv[u][:], op0=ALU.mult, op1=ALU.add)\
                    .then_inc(s["c_q"], 1)
                v.tensor_tensor(qk[u][:, 1].rearrange("n h d -> n (h d)"), ps[:, 4, C:2 * C], row("qk_b", C, C), ALU.add)\
                    .then_inc(s["c_k"], 1)

            def front_kdiag(b, u):
                dve.wait_ge(s["c_kT"], b + 1)
                for r in range(3):
                    rows = slice(32 * r, 32 * r + 32)
                    ins = v.tensor_copy(kdiag[u][rows, :, r], kxT[u][rows])
                ins.then_inc(s["c_kd"], 1)

            def maxima(b, u, e):
                dve.wait_ge(s["c_S"], 2 * b + e + 1)
                v.tensor_reduce(nmax[u][:, 8 * e:8 * e + 8],
                                ps[:, 2 * e:2 * e + 2, :].rearrange("n t (r k) -> n (t r) k", r=4), AX.X, ALU.max,
                                negate=True).then_inc(s["c_max"], 1)

            def split_max(b, u):
                m = nmax[u][:].rearrange("n (t r) -> n r t", r=4)
                dve.wait_ge(s["c_max"], 2 * b + 2)
                v.tensor_scalar(nm[u][:, :, 0:4].bitcast(F32R), m, valid[:, bass.ds(b, 1)], None, ALU.mult)\
                    .then_inc(s["c_nm"], 1)
                dve.wait_ge(s["c_nm"], 2 * b + 1)
                v.scalar_tensor_tensor(out=nm[u][:, :, 4:8].bitcast(F32R), in0=m, scalar=valid[:, bass.ds(b, 1)],
                                       in1=nm[u][:, :, 0:4], op0=ALU.mult, op1=ALU.subtract).then_inc(s["c_nm"], 1)

            def turned_max(b, u):
                dve.wait_ge(s["c_NT"], b + 1)
                for r in range(4):
                    rows = slice(32 * r, 32 * r + 32)
                    ins = v.tensor_copy(nmdiag[u][rows, r], ps[rows, 4, 256:256 + N])
                    if r % 2:
                        ins.then_inc(s["c_nmT"], 1)

            def reciprocals(b, u):
                dve.wait_ge(s["c_T2"], b + 1)
                v.reciprocal(rden[u][:], ps[:, 5, 0:256].rearrange("n (h z) -> n h z", z=16)[:, :, HD]).then_inc(s["c_rden"], 1)

            def normalise(b, u):
                o = ps[:, 5, 0:256].rearrange("n (h z) -> n h z", z=16)
                dve.wait_ge(s["c_rden"], b + 1)
                v.tensor_tensor(on[u][:], o[:, :, 0:HD], rden[u][:].unsqueeze(2).broadcast_to((N, 16, HD)), ALU.mult)\
                    .then_inc(s["c_on"], 1)

            def turned_o(b, u):
                dve.wait_ge(s["c_T3"], b + 1)
                v.tensor_copy(onT[u][:], ps[:, 4, 0:N]).then_inc(s["c_onT"], 1)

            def statistics_1(b):
                dve.wait_ge(s["c_res"], b + 1)
                settled(dve)
                v.bn_stats(bn_c[:], batch(xs, b)).then_inc(s["c_st"], 1)

            def statistics_2(b):
                dve.wait_ge(s["c_st"], 4 * b + 1)
                settled(dve)
                v.bn_aggr(agg_c[:], bn_c[:]).then_inc(s["c_st"], 1)

            def statistics_3(b):
                dve.wait_ge(s["c_st"], 4 * b + 2)
                v.tensor_scalar(var_eps[:, 3, bass.ds(b, 1)], agg_c[:, 1:2], EPS, None, ALU.add).then_inc(s["c_st"], 1)
                v.tensor_copy(mean[:, 1, bass.ds(b, 1)], agg_c[:, 0:1]).then_inc(s["c_st"], 1)

            def next_statistics(b):
                statistics_1(b)
                statistics_2(b)
                statistics_3(b)

            def step(b, u, end=True, back=True, front=True, ahead=True, x_ahead=True):
                maxima(b, u, 0)
                maxima(b, u, 1)
                split_max(b, u)
                if x_ahead:
                    front_x(b + 3, 1 - u)
                elif not ahead:
                    d_norm(b - (B - 2))
                turned_max(b, u)
                if end:
                    statistics_1(b - 2)
                if front:
                    front_kdiag(b + 1, 1 - u)
                if ahead:
                    front_qk(b + 2, u)
                if back:
                    reciprocals(b - 1, 1 - u)
                if end:
                    statistics_2(b - 2)
                if back:
                    normalise(b - 1, 1 - u)
                if end:
                    statistics_3(b - 2)

            dve.wait_ge(s["c_pow"], 1)
            front_x(0, 0)
            front_x(1, 1)
            b_residual(1)
            front_x(2, 0)
            front_qk(0, 0)
            dve.wait_ge(s["diag_ok"], 4)
            b_residual(2)
            front_kdiag(0, 0)
            front_qk(1, 1)
            step(0, 0, end=False, back=False)
            b_residual(3)
            dve.wait_ge(s["c_pow"], 3)
            step(1, 1, end=False)
            dve.wait_ge(s["c_pow"], 4)
            with dve.Fori(0, B // 2 - 3) as i:
                step(2 * i + 2, 0)
                step(2 * i + 3, 1)
            step(B - 4, 0)
            step(B - 3, 1, x_ahead=False)
            step(B - 2, 0, ahead=False, x_ahead=False)
            step(B - 1, 1, front=False, ahead=False, x_ahead=False)
            reciprocals(B - 1, 1)
            normalise(B - 1, 1)
            d_norm(2)
            next_statistics(B - 2)
            turned_o(B - 1, 1)
            dve.wait_ge(s["c_pr"], B)
            v.tensor_copy(attn[1][:], ps[:, 4, 2 * N:2 * N + C]).then_inc(s["c_at"], 1)
            next_statistics(B - 1)
            d_norm(3)
            for g in range(3):
                d_residual(g, 0, G)
            d_residual(3, 0, 2)
            d_residual(3, 2, 2)

        @block.gpsimd
        def _(pool):
            p = nc.gpsimd
            p.memset(ident[:], 0.0).then_inc(s["ident_ok"], 1)
            pool.wait_ge(s["ident_ok"], 1)
            p.affine_select(out=ident[:], in_=ident[:], compare_op=ALU.not_equal, fill=1.0, base=0,
                            pattern=[[-1, 128]], channel_multiplier=1).then_inc(s["ident_ok"], 1)
            p.memset(mask_rows[:], 0).then_inc(s["rows_ok"], 1)

            p.memset(upto[:], 1.0).then_inc(s["upto_ok"], 1)
            pool.wait_ge(s["upto_ok"], 1)
            p.affine_select(out=upto[:], in_=upto[:], compare_op=ALU.is_ge, fill=0.0, base=0,
                            pattern=[[1, 128]], channel_multiplier=-1).then_inc(s["upto_ok"], 1)

            def root(k, g, signal):
                if k < 3:
                    pool.wait_ge(s["stats_ok"], stats_end(k, g))
                else:
                    pool.wait_ge(s["c_st"], 4 * G * (g + 1))
                pool.wait_ge(s["half_ok"], 1)
                p.tensor_tensor(rstd[:, k, G * g:G * g + G], var_eps[:, k, G * g:G * g + G], half[:, 0:G], ALU.pow)\
                    .then_inc(signal, 1)

            def bias_add(g, bias, signal):
                b = G * g
                p.tensor_tensor(xb[:, b:b + G], xs[:, b:b + G], bias.unsqueeze(1).broadcast_to((N, G, C)), ALU.add)\
                    .then_inc(signal, 1)

            def norm(k, g, p_):
                root(k, g, s[p_ + "pow"])
                pool.wait_ge(s[p_ + "pow"], g + 1)
                if g > 1:
                    pool.wait_ge(s[p_ + "T"], g - 1)
                elif k == 1:
                    pool.wait_ge(s["a_T"], g + 3)
                for j in range(G):
                    b = G * g + j
                    ins = p.tensor_scalar(xn[g % 2][:, j], xs[:, b], rstd[:, k, b:b + 1], 0.0, ALU.mult, ALU.add)
                ins.then_inc(s[p_ + "xn"], 1)

            norm(0, 0, "a_")
            pool.wait_ge(s["ident_ok"], 2)
            pool.wait_ge(s["w_film"], 16)
            p.tensor_scalar(bcol[:], ident[:], 0.0, col("cols0", COL["v_b"]), ALU.mult, ALU.add).then_inc(s["bcol_ok"], 1)
            norm(0, 1, "a_")
            pool.wait_ge(s["bias_ok"], 1)
            bias_add(0, bias_a[:], s["a_xb"])
            norm(0, 2, "a_")
            bias_add(1, bias_a[:], s["a_xb"])
            norm(0, 3, "a_")
            bias_add(2, bias_a[:], s["a_xb"])
            bias_add(3, bias_a[:], s["a_xb"])

            for u in range(2):
                p.memset(vx[u][:], 0.0).then_inc(s["c_vinit"], 1)
                p.memset(nm[u][:], 0.0).then_inc(s["c_vinit"], 1)
                p.memset(nmdiag[u][:].bitcast(F32), 0.0).then_inc(s["c_vinit"], 1)
            pool.wait_ge(s["c_vinit"], 6)
            for u in range(2):
                for k in range(2):
                    z = vx[u][:].rearrange("n (a z) -> n a z", z=64)[:, :, 48 * k + HD:48 * k + HD + 1]
                    p.memset(z, 1.0).then_inc(s["c_vinit"], 1)

            p.memset(eye[:], 0.0).then_inc(s["eye_ok"], 1)
            pool.wait_ge(s["eye_ok"], 1)
            p.affine_select(out=eye[:], in_=eye[:], compare_op=ALU.not_equal, fill=1.0, base=0,
                            pattern=[[1, B], [-1, B]], channel_multiplier=0).then_inc(s["eye_ok"], 1)

            def next_bias(g):
                pool.wait_ge(s["a_res"], G * (g + 1))
                bias_add(g, row("mlp_b2"), s["b_xb"])

            pool.wait_ge(s["rows_in"], 16)
            norm(1, 0, "b_")
            next_bias(0)
            pool.wait_ge(s["w_ada"], 16)
            p.tensor_scalar(bcol1[:], ident[:], 0.0, col("cols1", COL1["v_b"]), ALU.mult, ALU.add).then_inc(s["bcol_ok"], 1)
            for m in qdiag:
                p.memset(m[:].bitcast(F32), 0.0).then_inc(s["diag_ok"], 1)
            norm(1, 1, "b_")
            next_bias(1)
            pool.wait_ge(s["mask_in"], 32)
            p.tensor_scalar(mask_b[:].rearrange("p b n -> p (b n)"), mask_i[:].rearrange("p b n -> p (b n)"), 1.0, 0.0,
                            ALU.mult, ALU.add).then_inc(s["maskb_ok"], 1)
            norm(1, 2, "b_")
            next_bias(2)
            norm(1, 3, "b_")
            next_bias(3)
            pool.wait_ge(s["selc_ok"], 1)
            pool.wait_ge(s["mask_rows_in"], 64)
            p.tensor_scalar(mask_term[:], mask_rows[:], row_amp[:, 0:1], row_neg[:, 0:1], ALU.mult, ALU.add)\
                .then_inc(s["mterm_ok"], 1)
            pool.wait_ge(s["mterm_ok"], 1)
            p.tensor_tensor(sel[:], sel_f[:].unsqueeze(2).broadcast_to((128, 4, N)),
                            mask_term[:].unsqueeze(1).broadcast_to((128, 4, N)), ALU.add).then_inc(s["sel_ok"], 1)
            pool.wait_ge(s["eye_ok"], 2)
            pool.wait_ge(s["valid_ok"], 1)
            p.tensor_tensor(own[:], eye[:], valid[:].unsqueeze(2).broadcast_to((N, B, B)), ALU.mult)\
                .then_inc(s["own_ok"], 1)
            for m in kdiag:
                p.memset(m[:].bitcast(F32), 0.0).then_inc(s["diag_ok"], 1)

            def prepare(b, u, end=False, last_kdiag=False):
                settled(pool)
                p.tensor_tensor(qbv[u][:], row("qk_b"), valid[:, bass.ds(b, 1)].broadcast_to((N, C)), ALU.mult)\
                    .then_inc(s["c_qbv"], 1)
                one = first[:, bass.ds(b, 1)].broadcast_to((N, N))
                p.tensor_tensor(nofirst[u][:], ident[:], one, ALU.subtract).then_inc(s["c_first"], 1)
                p.tensor_tensor(gtmp[:, u], gate[:, bass.ds(b, 1), 0, :].rearrange("p a c -> p (a c)"), pbias1[:], ALU.mult)\
                    .then_inc(s["c_gp"], 1)
                if end:
                    residual_1(b - 4, u)
                pool.wait_ge(s["c_first"], b + 1)
                settled(pool)
                p.tensor_tensor(keep[u][:], nofirst[u][:], mask_b[:, bass.ds(b, 1), :].rearrange("p a n -> p (a n)"),
                                ALU.mult).then_inc(s["c_keep"], 1)
                if end:
                    residual_2(b - 4, u)
                pool.wait_ge(s["c_gp"], b + 1)
                settled(pool)
                p.tensor_tensor(batch(xb, b), batch(xs, b), gtmp[:, u], ALU.add).then_inc(s["c_xb"], 1)
                pool.wait_ge(s["c_keep"], b + 1)
                settled(pool)
                p.tensor_tensor(turn_k[u][:], keep[u][:], one, ALU.add).then_inc(s["c_turn"], 1)
                if last_kdiag:
                    front_kdiag(b - 1, 1 - u)
                if not isinstance(b, int) or b >= 2:
                    pool.wait_ge(s["c_ST"], 2 * b - 2)
                    settled(pool)
                p.tensor_copy(nm[u][:, :, MROW:32], own[:, bass.ds(b, 1), :].broadcast_to((N, 4, B))).then_inc(s["c_nv"], 1)

            def lower(b, u):
                for n, (hi, lo, signal) in enumerate(((slice(0, 2), slice(2, 4), "c_hiq"),
                                                      (slice(0, 4, 2), slice(1, 4, 2), "c_hik"))):
                    pool.wait_ge(s[signal], b + 1)
                    p.tensor_tensor(qkx[u][:, n, :, lo].bitcast(F32R), qk[u][:, n].unsqueeze(2).broadcast_to((N, H, 2, HD)),
                                    qkx[u][:, n, :, hi], ALU.subtract).then_inc(s["c_lo"], 1)

            def front_kdiag(b, u):
                pool.wait_ge(s["c_kT"], b + 1)
                p.tensor_tensor(kdiag[u][:, :, 3], kxT[u][:], quarter[:].unsqueeze(1).broadcast_to((128, 4, N)), ALU.mult)\
                    .then_inc(s["c_kd3"], 1)

            def residual_1(b, u):
                pool.wait_ge(s["c_at"], b + 1)
                settled(pool)
                p.tensor_tensor(gated[u][:], attn[u][:], gate[:, bass.ds(b, 1), 0, :].rearrange("p a c -> p (a c)"), ALU.mult)\
                    .then_inc(s["c_ga"], 1)

            def residual_2(b, u):
                pool.wait_ge(s["c_ga"], b + 1)
                pool.wait_ge(s["c_xb"], b + 1)
                settled(pool)
                p.tensor_tensor(batch(xs, b), gated[u][:], batch(xb, b), ALU.add).then_inc(s["c_res"], 1)

            def step(b, u, end=True, front=True, ahead=True):
                if front:
                    lower(b + 1, 1 - u)
                if ahead:
                    prepare(b + 2, u, end, True)
                else:
                    if end:
                        residual_1(b - 2, u)
                        residual_2(b - 2, u)
                    if front:
                        front_kdiag(b + 1, 1 - u)

            pool.wait_ge(s["own_ok"], 1)
            pool.wait_ge(s["gate_in"], 16)
            pool.wait_ge(s["pbias_ok"], 1)
            pool.wait_ge(s["valid_ok"], 1)
            pool.wait_ge(s["c_vinit"], 10)
            pool.wait_ge(s["maskb_ok"], 1)
            root(2, 0, s["c_pow"])
            prepare(0, 0)
            root(2, 1, s["c_pow"])
            lower(0, 0)
            prepare(1, 1)
            front_kdiag(0, 0)
            root(2, 2, s["c_pow"])
            step(0, 0, end=False)
            step(1, 1, end=False)
            root(2, 3, s["c_pow"])
            with pool.Fori(0, B // 2 - 3) as i:
                step(2 * i + 2, 0)
                step(2 * i + 3, 1)
            step(B - 4, 0)
            root(3, 0, s["d_pow"])
            step(B - 3, 1)
            root(3, 1, s["d_pow"])
            step(B - 2, 0, ahead=False)

            def d_bias(g):
                b = G * g
                pool.wait_ge(s["c_res"], b + G)
                p.tensor_tensor(gtmp[:], gate[:, b:b + G, 1, :], row("fc2_b").unsqueeze(1).broadcast_to((N, G, C)),
                                ALU.mult).then_inc(s["d_gp"], 1)
                pool.wait_ge(s["d_gp"], g + 1)
                p.tensor_tensor(xb[:, b:b + G], xs[:, b:b + G], gtmp[:], ALU.add).then_inc(s["d_xb"], 1)
                pool.wait_ge(s["d_xb"], g + 1)

            step(B - 1, 1, front=False, ahead=False)
            root(3, 2, s["d_pow"])
            residual_1(B - 2, 0)
            residual_2(B - 2, 0)
            d_bias(0)
            residual_1(B - 1, 1)
            residual_2(B - 1, 1)
            root(3, 3, s["d_pow"])
            for g in range(1, 4):
                d_bias(g)


def kernel(**inputs):
    import numpy as np
    import concourse.bacc as bacc
    from concourse.bass_utils import run_bass_kernel_spmd

    a = {k: np.asarray(v) for k, v in inputs.items()}
    l0 = {k[8:]: v for k, v in a.items() if k.startswith("L0_cond_")}
    l1 = {k[8:]: v for k, v in a.items() if k.startswith("L1_cond_")}

    def columns(*vectors):
        cols = np.concatenate([v.reshape(-1, 128) for v in vectors]).T
        return np.concatenate([cols, np.zeros((128, 16 - cols.shape[1]), np.float32)], axis=1)

    packed = {
        "cond": a["cond_1024"].T, "film1": l0["film1_w"], "film2": l0["film2_w"],
        "cols0": columns(l0["q_b"], l0["k_b"], l0["v_b"], l0["norm1_w"], l0["norm2_w"], l0["film1_b"],
                         l0["film2_b"], l0["mlp_b1"]),
        "q": l0["q_w"], "k": l0["k_w"], "vt": l0["v_w"].T, "proj": l0["proj_w"], "mlp1": l0["mlp_w1"],
        "mlp2": l0["mlp_w2"].reshape(FC, 128, C).transpose(1, 0, 2).reshape(128, F),
        "ada": l1["ada_w"].T,
        "cols1": columns(l1["ada_b"], l1["qkv_b"][2 * C:], l1["fc1_b"]),
        "qkv": l1["qkv_w"].T,
        "proj1": l1["proj_w"].T, "fc1": l1["fc1_w"].T,
        "fc2": l1["fc2_w"].T.reshape(FC, 128, C).transpose(1, 0, 2).reshape(128, F),
    }
    ada_b = l1["ada_b"].reshape(6, C)
    in_map = {
        "x": np.ascontiguousarray(a["x"].transpose(1, 0, 2)),
        "weights": np.ascontiguousarray(np.concatenate([packed[n] for n, size in _W if size], axis=1)),
        "rows": np.concatenate([l0["proj_b"], l0["mlp_b2"], l1["qkv_b"][:2 * C], l1["proj_b"], l1["fc2_b"],
                                ada_b[2], ada_b[5]]),
        "mask": a["mask_BxS_bk1"].astype(np.int32),
        "mask_t": np.ascontiguousarray(a["mask_BxS_bk1"].T).astype(np.int32),
    }
    nc = bacc.Bacc("TRN2", target_bir_lowering=False, num_devices=1)
    aps = [nc.dram_tensor(n, v.shape, mybir.dt.from_np(v.dtype), kind="ExternalInput").ap() for n, v in in_map.items()]
    gates = nc.dram_tensor("gates", (B, 2 * C), F32, kind="Internal").ap()
    out = nc.dram_tensor("out", (N, B, C), F32, kind="ExternalOutput").ap()
    build(nc, *aps, gates, out)
    result = run_bass_kernel_spmd(nc, [in_map], core_ids=[0])
    return np.ascontiguousarray(result.results[0]["out"].transpose(1, 0, 2))
```
